# Optimizing a Trainium2 kernel written in Bass

```python
import numpy as np
import jax
import jax.numpy as jnp

def _softmax(x, axis=-1):
    return jax.nn.softmax(x, axis=axis)

def _gelu(x):
    return jax.nn.gelu(x, approximate=True)

def _silu(x):
    return jax.nn.silu(x)

def _sigmoid(x):
    return jax.nn.sigmoid(x)

def _layernorm(x, axis=-1, eps=1e-05):
    m = jnp.mean(x, axis=axis, keepdims=True)
    v = jnp.var(x, axis=axis, keepdims=True)
    return (x - m) / jnp.sqrt(v + eps)

def _scatter_add(tgt, idx, src, axis=0):
    return tgt.at[idx].add(src)

def _segment_sum(src, seg, n):
    return jax.ops.segment_sum(src, seg, n)
kernel_name = 'mk_metaformer_d1_conv_nhwc512_r4_04e763'

def setup_inputs(seed: int=0):
    np.random.seed(seed)
    _w = jnp.asarray

    def _rec_inputs():
        import jax
        import jax.numpy as jnp
        _gk = jax.random.key(seed)
        x = -0.0003957 + 1 * jax.random.normal(jax.random.fold_in(_gk, 1), (4, 32, 49, 128), jnp.float32)
        return x
    x = _rec_inputs()

    def _L0_conv_setup():
        import jax, jax.numpy as jnp
        import numpy as np
        ALPHA = 2.0
        V_TH = 1.0
        H = 8

        @jax.custom_vjp
        def atan_spike(x):
            return (x >= 0.0).astype(x.dtype)

        def _spike_fwd(x):
            return (atan_spike(x), x)

        def _spike_bwd(x, g):
            pi_half = jnp.asarray(np.pi / 2, x.dtype)
            grad = ALPHA / 2.0 / (1.0 + (pi_half * ALPHA * x) ** 2)
            return (g * grad,)
        atan_spike.defvjp(_spike_fwd, _spike_bwd)

        def lif(x_seq, w):
            sg = jax.nn.sigmoid(w)

            def step(v, x):
                h = v + (x - v) * sg
                s = atan_spike(h - V_TH)
                v_new = h * (1.0 - jax.lax.stop_gradient(s))
                return (v_new, s)
            v0 = jnp.zeros_like(x_seq[0])
            _, spikes = jax.lax.scan(step, v0, x_seq)
            return spikes
        key = jax.random.key(seed)
        ks = jax.random.split(key, 6)
        T, B, N, C = (4, 32, 49, 128)
        s = 0.02
        return {'x': jax.random.normal(ks[0], (T, B, N, C), dtype=jnp.float32), 'Wq': jax.random.normal(ks[1], (C, C), dtype=jnp.float32) * s, 'Wk': jax.random.normal(ks[2], (C, C), dtype=jnp.float32) * s, 'Wv': jax.random.normal(ks[3], (C, C), dtype=jnp.float32) * s, 'Wp': jax.random.normal(ks[4], (C, C), dtype=jnp.float32) * s, 'bp': jax.random.normal(ks[5], (C,), dtype=jnp.float32) * s, 'wq': jnp.zeros((), jnp.float32), 'wk': jnp.zeros((), jnp.float32), 'wv': jnp.zeros((), jnp.float32), 'wa': jnp.zeros((), jnp.float32), 'wp': jnp.zeros((), jnp.float32)}
    _L0_conv_all = _L0_conv_setup()
    _L0_conv_in = {k: v for k, v in _L0_conv_all.items() if k in ('Wq', 'Wk', 'Wv', 'Wp', 'bp', 'wq', 'wk', 'wv', 'wa', 'wp')}
    del _L0_conv_all

    def _L0_ffn_setup():
        import jax, jax.numpy as jnp
        import numpy as np
        B, L, D, H, E, K = (8, 2048, 128, 512, 8, 2)
        SCALE = 0.02
        key = jax.random.key(seed)
        ks = jax.random.split(key, 6)
        return {'x': jax.random.normal(ks[0], (B, L, D), dtype=jnp.float32), 'Wg': jax.random.normal(ks[1], (D, E), dtype=jnp.float32) * SCALE, 'W1': jax.random.normal(ks[2], (E, D, H), dtype=jnp.float32) * SCALE, 'b1': jax.random.normal(ks[3], (E, H), dtype=jnp.float32) * SCALE, 'W2': jax.random.normal(ks[4], (E, H, D), dtype=jnp.float32) * SCALE, 'b2': jax.random.normal(ks[5], (E, D), dtype=jnp.float32) * SCALE}
    _L0_ffn_all = _L0_ffn_setup()
    _L0_ffn_in = {k: v for k, v in _L0_ffn_all.items() if k in ('Wg', 'W1', 'b1', 'W2', 'b2')}
    del _L0_ffn_all
    return {'x': x, 'L0_conv_Wq': _L0_conv_in['Wq'], 'L0_conv_Wk': _L0_conv_in['Wk'], 'L0_conv_Wv': _L0_conv_in['Wv'], 'L0_conv_Wp': _L0_conv_in['Wp'], 'L0_conv_bp': _L0_conv_in['bp'], 'L0_conv_wq': _L0_conv_in['wq'], 'L0_conv_wk': _L0_conv_in['wk'], 'L0_conv_wv': _L0_conv_in['wv'], 'L0_conv_wa': _L0_conv_in['wa'], 'L0_conv_wp': _L0_conv_in['wp'], 'L0_ffn_Wg': _L0_ffn_in['Wg'], 'L0_ffn_W1': _L0_ffn_in['W1'], 'L0_ffn_b1': _L0_ffn_in['b1'], 'L0_ffn_W2': _L0_ffn_in['W2'], 'L0_ffn_b2': _L0_ffn_in['b2']}

def reference(x, L0_conv_Wq, L0_conv_Wk, L0_conv_Wv, L0_conv_Wp, L0_conv_bp, L0_conv_wq, L0_conv_wk, L0_conv_wv, L0_conv_wa, L0_conv_wp, L0_ffn_Wg, L0_ffn_W1, L0_ffn_b1, L0_ffn_W2, L0_ffn_b2):
    import jax
    import jax.numpy as jnp

    def _L0_conv_ref(x, Wq, Wk, Wv, Wp, bp, wq, wk, wv, wa, wp):
        import jax, jax.numpy as jnp
        import numpy as np
        ALPHA = 2.0
        V_TH = 1.0
        H = 8

        @jax.custom_vjp
        def atan_spike(x):
            return (x >= 0.0).astype(x.dtype)

        def _spike_fwd(x):
            return (atan_spike(x), x)

        def _spike_bwd(x, g):
            pi_half = jnp.asarray(np.pi / 2, x.dtype)
            grad = ALPHA / 2.0 / (1.0 + (pi_half * ALPHA * x) ** 2)
            return (g * grad,)
        atan_spike.defvjp(_spike_fwd, _spike_bwd)

        def lif(x_seq, w):
            sg = jax.nn.sigmoid(w)

            def step(v, x):
                h = v + (x - v) * sg
                s = atan_spike(h - V_TH)
                v_new = h * (1.0 - jax.lax.stop_gradient(s))
                return (v_new, s)
            v0 = jnp.zeros_like(x_seq[0])
            _, spikes = jax.lax.scan(step, v0, x_seq)
            return spikes
        T, B, N, C = x.shape
        d = C // H
        scale = d ** (-0.5)
        xf = x.reshape(T * B, N, C)

        def qkv(W, w_lif):
            y = lif(xf @ W.T, w_lif)
            return y.reshape(T, B, N, H, d).transpose(0, 1, 3, 2, 4)
        q = qkv(Wq, wq)
        k = qkv(Wk, wk)
        v = qkv(Wv, wv)
        attn = jnp.einsum('tbhnd,tbhmd->tbhnm', q, k) * scale
        y = jnp.einsum('tbhnm,tbhmd->tbhnd', attn, v)
        y = y.swapaxes(3, 4).reshape(T, B, N, C)
        y = lif(y, wa)
        out = lif(y.reshape(T * B, N, C) @ Wp.T + bp, wp)
        return out.reshape(T, B, N, C)

    def _L0_ffn_ref(x, Wg, W1, b1, W2, b2):
        import jax, jax.numpy as jnp
        import numpy as np
        B, L, D, H, E, K = (8, 2048, 128, 512, 8, 2)
        SCALE = 0.02
        b, l, d = x.shape
        xt = x.reshape(-1, d)
        T = xt.shape[0]
        gate = jax.nn.softmax(xt @ Wg, axis=-1)
        topv, topi = jax.lax.top_k(gate, K)
        topv = topv / (jnp.sum(topv, axis=-1, keepdims=True) + 1e-06)
        scores = jnp.zeros((T, E), dtype=xt.dtype).at[jnp.arange(T)[:, None], topi].set(topv)
        out = jnp.zeros_like(xt)
        for e in range(E):
            h = jax.nn.gelu(xt @ W1[e] + b1[e], approximate=False)
            ye = h @ W2[e] + b2[e]
            out = out + ye * scores[:, e:e + 1]
        return out.reshape(b, l, d)

    def _gn(v, G=32, eps=1e-05):
        B_, H_, W_, C_ = v.shape
        g = v.reshape(B_, H_, W_, G, C_ // G)
        m = jnp.mean(g, axis=(1, 2, 4), keepdims=True)
        s = jnp.var(g, axis=(1, 2, 4), keepdims=True)
        return ((g - m) / jnp.sqrt(s + eps)).reshape(v.shape)

    def _ln_c(v, eps=1e-06):
        m = jnp.mean(v, axis=-1, keepdims=True)
        s = jnp.var(v, axis=-1, keepdims=True)
        return (v - m) / jnp.sqrt(s + eps)

    def _ln_t(v, eps=1e-05):
        m = jnp.mean(v, axis=-1, keepdims=True)
        s = jnp.var(v, axis=-1, keepdims=True)
        return (v - m) / jnp.sqrt(s + eps)

    def _to_tokens(v):
        B_, H_, W_, C_ = v.shape
        return v.reshape(B_, H_ * W_, C_)

    def _from_tokens(t, like):
        return t.reshape(like.shape)
    x = x + _L0_conv_ref(_ln_c(x), L0_conv_Wq, L0_conv_Wk, L0_conv_Wv, L0_conv_Wp, L0_conv_bp, L0_conv_wq, L0_conv_wk, L0_conv_wv, L0_conv_wa, L0_conv_wp)
    t = _to_tokens(x)
    t = t + _L0_ffn_ref(_ln_t(t), L0_ffn_Wg, L0_ffn_W1, L0_ffn_b1, L0_ffn_W2, L0_ffn_b2)
    x = _from_tokens(t, x)
    return x

_drawn_inputs = setup_inputs


def setup_inputs(seed=0):
    import zlib

    import numpy as np

    out = dict(_drawn_inputs(seed))
    spreads = {}
    factors = {'L0_ffn_b1': 8.0, 'L0_ffn_b2': 3.868}
    for name, (base, spread) in spreads.items():
        noise = np.random.default_rng([zlib.crc32(name.encode()), seed]).standard_normal(out[name].shape)
        drawn = base * np.exp(spread * noise) if base else spread * noise
        out[name] = jnp.asarray(drawn.astype(out[name].dtype))
    for name, factor in factors.items():
        out[name] = (out[name] * factor).astype(out[name].dtype)
    return out
```

```python
from contextlib import ExitStack

import concourse.bass as bass
from concourse import mybir

ALU = mybir.AluOpType
ACT = mybir.ActivationFunctionType
AX = mybir.AxisListType
F32 = mybir.dt.float32
BF16 = mybir.dt.bfloat16
F16 = mybir.dt.float16


class Steps:

    def __init__(self, engine, semaphore):
        self.engine, self.semaphore, self.base, self.count = engine, semaphore, 0, 0

    def mark(self, instruction):
        instruction.then_inc(self.semaphore, 1)
        self.count += 1
        return self.count

    def wait(self, mark):
        self.engine.wait_ge(self.semaphore, self.base + mark)


def metaformer_block(nc, x, Wq, Wk, Wv, Wp, bp, lif_w, Wg, W1, b1, W2, b2, out):
    T, B, N, C = x.shape
    TB = T * B
    E, _, HID = W1.shape
    HB = HID // 128
    HEADS = 8
    D = C // HEADS
    NPAD = 64
    PAIRS = TB // 2
    LN1_EPS, LN2_EPS, GATE_EPS = 1e-6, 1e-5, 1e-6
    TOK = TB * N
    TILES = TOK // 128
    R = 7
    G = TILES // R
    SB = 8
    BLOCKS = TB // SB
    BC = SB * N
    LAG = 7
    SLOTS = BLOCKS + LAG
    assert C == 128 and TB == 128 and HID % 128 == 0 and TOK % (128 * R) == 0 and N <= NPAD and BC <= 512
    W = R * 128
    CUTS = [(0, 4), (4, R)]
    BT = BLOCKS // T

    x_v = x.rearrange("t b n c -> (t b n) c").rearrange("(k p) c -> p k c", p=128)
    out_v = out.rearrange("t b n c -> (t b n) c").rearrange("(k p) c -> p k c", p=128)

    def norm1_block(g):
        return W * g // BC

    def norm2_block(g):
        return (W * (g + 1) - 1) // BC

    norm1_slot = {g: norm1_block(g) - 3 for g in range(G)}
    norm2_slot = {g: norm2_block(g) + LAG + 1 for g in range(G)}
    END = max(norm2_slot.values()) + 2

    def ring_items(slot):
        got = []
        for g in range(G):
            if (norm1_slot[g] + 1 if norm1_slot[g] > -1 else -1) == slot:
                got += [("turn", 0, g, c) for c in range(2)]
        if slot + 1 < BLOCKS:
            got += [("qkv", w, slot + 1, 0) for w in range(3)]
        if 0 <= slot + 1 - LAG < BLOCKS:
            got.append(("qkv", 3, slot + 1 - LAG, 0))
        for g in range(G):
            if norm2_slot[g] + 1 == slot:
                got += [("turn", 1, g, c) for c in range(2)]
        return got

    def norms(slot):
        return ([(0, g) for g in range(G) if max(norm1_slot[g], -1) == slot]
                + [(1, g) for g in range(G) if norm2_slot[g] == slot])

    norm_order = [x for s in range(-1, END) for x in norms(s)]
    norm_rank = {x: i for i, x in enumerate(norm_order)}
    item_rank, ring = {}, {}
    for s in range(-1, END):
        ring[s] = ring_items(s)
        for it in ring[s]:
            item_rank[it] = len(item_rank)

    ctx = ExitStack()
    with ctx:
        def sb(name, shape, dt=F32):
            return ctx.enter_context(nc.sbuf_tensor(name, shape, dt))

        def sem(name):
            return ctx.enter_context(nc.semaphore(name))

        PS = ctx.enter_context(nc.psum_tensor("PS", [128, 8, 512], F32))
        RING, KVT_BANK, KV_BANK, Y_BANK, PERM_BANK = 0, 2, 3, 5, 7

        X = sb("X", [128, TILES, C])
        XD = sb("XD", [128, R, C])
        XN = sb("XN", [128, R, C])
        xT = sb("xT", [128, TOK])
        spikes = [sb(f"spikes{i}", [128, 3, SB, NPAD], BF16) for i in range(2)]
        H = [sb(f"H{i}", [128, SB, 4, N]) for i in range(3)]
        U = sb("U", [128, 4, N])
        VV = sb("VV", [128, 4, N])
        OM = sb("OM", [128, 4, N])
        KVT = [sb(f"KVT{i}", [128, 2, 4, 128], BF16) for i in range(2)]
        KV = [sb(f"KV{i}", [128, 4, 2, 128], BF16) for i in range(2)]
        Y = sb("Y", [128, C, PAIRS], F16)
        HY = sb("HY", [128, N, B])
        VY = sb("VY", [128, N, B])
        ysp = [sb(f"ysp{i}", [128, B, N], BF16) for i in range(2)]
        osp = sb("osp", [128, TOK], BF16)
        shift = sb("shift", [128, 2, 304], F16)
        mask = sb("mask", [128, HEADS, D])
        identf = sb("identf", [128, 128])
        identb = sb("identb", [128, 128], BF16)
        ones = HY[:].rearrange("p n b -> p (n b)")[:, 0:608].rearrange("p (a b) -> p a b", a=2)
        wrow = HY[:].rearrange("p n b -> p (n b)")[:, 608:1120].rearrange("p (a b) -> p a b", a=4)
        wT = sb("wT", [128, 4, C])
        wpT = sb("wpT", [128, 3, C], BF16)
        wres = VY[:].rearrange("p n b -> p (n b)")[:, 0:2 * C].rearrange("p (a b) -> p a b", a=2)
        bp_c = sb("bp_c", [128, 1])
        bsg = sb("bsg", [128, 1])
        lw = sb("lw", [128, 5])
        sg = sb("sg", [128, 5])
        osg = sb("osg", [128, 5])
        stats = sb("stats", [128, TILES, 6])
        ln = sb("ln", [128, 2, 6, TILES])
        Wg_s = sb("Wg_s", [128, E])
        W1_s = sb("W1_s", [128, E, HID])
        W2_s = sb("W2_s", [128, E, HB, C])
        b1r = sb("b1r", [E * HB, 128])
        b1c = sb("b1c", [128, E * HB])
        b2b = sb("b2b", [128, E, C])
        g1 = sb("g1", [128, 6, TILES])
        rank = sb("rank", [128, E])
        score = sb("score", [128, TILES, E])
        lneps1 = sb("lneps1", [128, 1])
        lneps2 = sb("lneps2", [128, 1])
        free = Y[:].rearrange("p c n -> p (c n)").bitcast(F32)
        hid = [free[:, i * HB * 512:(i + 1) * HB * 512].rearrange("p (b c) -> p b c", b=HB) for i in range(2)]
        gt = osp[:].bitcast(F32)[:, 0:6 * TILES * E].rearrange("p (k n e) -> p k n e", k=6, e=E)
        XD2 = H[0][:].rearrange("p s w n -> p (s w n)")[:, 0:1024].rearrange("p (k a c) -> p k a c", k=2, c=C)

        x_in = [sem(f"x_in{g}") for g in range(G)]
        x_ready = sem("x_ready")
        w_in = sem("w_in")
        ffn_in = sem("ffn_in")
        consts = sem("consts")
        dve = sem("dve_step")
        actst = sem("act_step")
        pools = sem("pool_step")
        lw_exp = sem("lw_exp")
        sg_ready = sem("sg_ready")
        w_turned = sem("w_turned")
        w_ready = sem("w_ready")
        wp_split = sem("wp_split")
        var_ready = sem("var_ready")
        std_ready = sem("std_ready")
        rstd_ready = sem("rstd_ready")
        xn_ready = sem("xn_ready")
        xt_turned = sem("xt_turned")
        ring_done = sem("ring_done")
        ring_copied = sem("ring_copied")
        block_done = sem("block_done")
        kvt_turned = sem("kvt_turned")
        kvt_copied = sem("kvt_copied")
        kv_done = sem("kv_done")
        kv_masked = sem("kv_masked")
        y_done = sem("y_done")
        y_copied = sem("y_copied")
        perm_done = sem("perm_done")
        perm_copied = sem("perm_copied")
        hy_used = sem("hy_used")
        ysp_ready = sem("ysp_ready")
        osp_ready = sem("osp_ready")
        osp_turned = sem("osp_turned")
        res_added = sem("res_added")
        logits_done = sem("logits_done")
        gate_in = sem("gate_in")
        gate_exp = sem("gate_exp")
        score_ready = sem("score_ready")
        up_done = sem("up_done")
        gelu_done = sem("gelu_done")
        down_done = sem("down_done")
        y_added = sem("y_added")
        out_ready = sem("out_ready")
        stored = sem("stored")

        block = ctx.enter_context(nc.Block())
        PERM = [(n, min(n + 14, N)) for n in range(0, N, 14)]

        @block.sync
        def _(sp):
            for g in range(G):
                sp.dma_start(X[:, R * g:R * g + R, :], x_v[:, R * g:R * g + R, :]).then_inc(x_in[g], 16)
            sp.dma_start(W1_s[:], W1.rearrange("e c h -> c e h")).then_inc(ffn_in, 16)
            sp.dma_start(W2_s[:], W2.rearrange("e (b h) c -> h e b c", h=128)).then_inc(ffn_in, 16)
            sp.dma_start(b1r[:], b1.rearrange("e (b h) -> (e b) h", h=128)).then_inc(ffn_in, 16)
            sp.dma_start(b2b[:], b2.rearrange("e c -> (e c)").partition_broadcast(128)
                         .rearrange("p (e c) -> p e c", c=C)).then_inc(ffn_in, 16)
            for g in range(G):
                sp.wait_ge(x_in[g], 16)
                sp.sem_inc(x_ready, 1)
            for g in range(G):
                sp.wait_ge(out_ready, g + 1)
                sp.dma_start(out_v[:, R * g:R * g + R, :], X[:, R * g:R * g + R, :]).then_inc(stored, 16)
            sp.wait_ge(stored, 16 * G)

        @block.gpsimd
        def _(pool):
            steps = Steps(pool, pools)
            steps.mark(pool.memset(ones, 1.0))
            steps.mark(pool.memset(spikes[0][:, :, :, N:NPAD], 0.0))
            steps.mark(pool.memset(spikes[1][:, :, :, N:NPAD], 0.0))
            pool.memset(Y[:], 0.0).then_inc(consts, 1)
            steps.wait(3)
            one = ones[:, 0, 0:128]
            pool.affine_select(out=identf[:], in_=one, compare_op=ALU.is_equal, fill=0.0, base=0,
                               pattern=[[-1, 128]], channel_multiplier=1).then_inc(consts, 1)
            pool.affine_select(out=identb[:], in_=one, compare_op=ALU.is_equal, fill=0.0, base=0,
                               pattern=[[-1, 128]], channel_multiplier=1).then_inc(consts, 1)
            pool.affine_select(out=shift[:], in_=ones, compare_op=ALU.is_equal, fill=0.0, base=127,
                               pattern=[[-64, 2], [-1, 304]], channel_multiplier=1).then_inc(pools, 1)
            steps.count += 1
            steps.wait(steps.count)
            pool.memset(shift[64:128, 0, :], 0.0).then_inc(consts, 1)
            pool.memset(shift[0:64, 1, :], 0.0).then_inc(consts, 1)
            pool.wait_ge(consts, 5)
            m1 = pool.affine_select(out=mask[:], in_=ones[:, 0, 0:128].rearrange("p (h d) -> p h d", d=D),
                                    compare_op=ALU.is_ge, fill=0.0, base=0,
                                    pattern=[[-D, HEADS], [0, D]], channel_multiplier=1)
            m = steps.mark(m1)
            steps.wait(m)
            pool.affine_select(out=mask[:], in_=mask[:], compare_op=ALU.is_ge, fill=0.0, base=D - 1,
                               pattern=[[D, HEADS], [0, D]], channel_multiplier=-1).then_inc(consts, 1)
            pool.iota(rank[:], pattern=[[-1, E]], base=E, channel_multiplier=0,
                      allow_small_or_imprecise_dtypes=True).then_inc(consts, 1)

            for k, (phase, g) in enumerate(norm_order):
                rows = X[:, R * g:R * g + R, :]
                bc = lambda row: ln[:, phase, row, R * g:R * g + R].unsqueeze(2).to_broadcast([128, R, C])
                pool.wait_ge(rstd_ready, k + 1)
                if k:
                    pool.wait_ge(xn_ready, k)
                m = steps.mark(pool.tensor_tensor(XD[:], rows, bc(0), ALU.subtract))
                steps.wait(m)
                if k:
                    pool.wait_ge(xt_turned, k)
                pool.tensor_tensor(XN[:], XD[:], bc(5), ALU.mult).then_inc(xn_ready, 1)

        NCONST = 7

        @block.scalar
        def _(act):
            with nc.allow_non_contiguous_dma(reason="a column of biases"):
                for i, w in enumerate((Wq, Wk, Wv, Wp)):
                    act.dma_start(wrow[:, i, :], w).then_inc(w_in, 16)
                act.dma_start(lw[:], lif_w.partition_broadcast(128)).then_inc(w_in, 16)
                act.dma_start(bp_c[:], bp.rearrange("(c a) -> c a", a=1)).then_inc(w_in, 16)
                act.dma_start(Wg_s[:], Wg).then_inc(w_in, 16)
            act.wait_ge(w_in, 16 * 7)
            nc.scalar.activation(sg[:], lw[:], ACT.Exp, scale=-1.0).then_inc(lw_exp, 1)
            act.wait_ge(w_turned, 1)
            nc.scalar.activation(wT[:].rearrange("p a c -> p (a c)"), PS[:, 0, :], ACT.Copy).then_inc(w_ready, 1)
            act.wait_ge(sg_ready, 1)

            def spread(phase, g):
                act.wait_ge(var_ready, norm_rank[phase, g] + 1)
                cols = slice(R * g, R * g + R)
                nc.scalar.activation(ln[:, phase, 4, cols], ln[:, phase, 3, cols], ACT.Sqrt,
                                     bias=(lneps1, lneps2)[phase][:], scale=1.0 / C).then_inc(std_ready, 1)

            def copy_item(item):
                kind, w, b, c = item
                n = item_rank[item]
                act.wait_ge(ring_done, n + 1)
                bank = PS[:, RING + n % 2, :]
                if kind == "turn":
                    k0, k1 = (R * b + x for x in CUTS[c])
                    nc.scalar.activation(xT[:, 128 * k0:128 * k1], bank[:, 0:128 * (k1 - k0)],
                                         ACT.Copy).then_inc(ring_copied, 1)
                    return
                slot = b + (LAG if w == 3 else 0)
                if slot >= 3:
                    act.wait_ge(block_done, slot - 2)
                dst = H[slot % 3][:, :, w, :]
                src = bank[:, 0:BC].rearrange("p (s n) -> p s n", n=N)
                if w == 3:
                    nc.scalar.activation(dst, src, ACT.Identity, scale=sg[:, 4:5],
                                         bias=bsg[:, 0:1]).then_inc(ring_copied, 1)
                else:
                    nc.scalar.activation(dst, src, ACT.Copy, scale=sg[:, w:w + 1]).then_inc(ring_copied, 1)

            def copy_kvt(i):
                act.wait_ge(kvt_turned, i + 1)
                if i >= 2:
                    act.wait_ge(kv_done, i - 1)
                nc.scalar.activation(KVT[i % 2][:].rearrange("p w a c -> p (w a c)"), PS[:, KVT_BANK, :].bitcast(BF16),
                                     ACT.Copy).then_inc(kvt_copied, 1)

            def copy_y(i):
                for half in range(2):
                    act.wait_ge(y_done, 2 * i + half + 1)
                    for par in range(2):
                        rows = slice(64 * par, 64 * par + N)
                        src = PS[rows, Y_BANK + half, :].rearrange("p (i h c) -> p i h c", i=2, h=2)[:, :, par, :]
                        p0 = 4 * i + 2 * half
                        nc.scalar.activation(Y[rows, :, p0:p0 + 2].rearrange("p c i -> p i c"), src,
                                             ACT.Copy, scale=D ** -0.5).then_inc(y_copied, 1)

            def copy_perm(t):
                if t:
                    act.wait_ge(hy_used, t)
                for c, (n0, n1) in enumerate(PERM):
                    act.wait_ge(perm_done, len(PERM) * t + c + 1)
                    k = n1 - n0
                    src = PS[:, PERM_BANK, 0:k * B].rearrange("p (n h j) -> p n h j", n=k, h=2)
                    dst = HY[:, n0:n1, :].rearrange("p n (j h) -> p n h j", h=2)
                    nc.scalar.activation(dst, src, ACT.Copy, scale=sg[:, 3:4]).then_inc(perm_copied, 1)

            for slot in range(-1, END):
                if slot < 0:
                    for x_ in norms(slot):
                        spread(*x_)
                for it in ring[slot]:
                    copy_item(it)
                if 1 <= slot <= BLOCKS:
                    copy_kvt(slot - 1)
                    copy_y(slot - 1)
                    if slot % BT == 0:
                        copy_perm(slot // BT - 1)
                if slot >= 0:
                    for x_ in norms(slot):
                        spread(*x_)
            act.wait_ge(gate_in, 1)
            nc.scalar.activation(gt[:, 1], gt[:, 0], ACT.Exp).then_inc(gate_exp, 1)
            k = 0
            for g in range(G):
                for c0, c1 in CUTS:
                    for e in range(E):
                        for hb in range(HB):
                            act.wait_ge(up_done, k + 1)
                            if k >= 2 * HB:
                                act.wait_ge(down_done, k // HB - 1)
                            cols = slice(0, 128 * (c1 - c0))
                            nc.scalar.activation(hid[(k // HB) % 2][:, hb, cols], PS[:, hb, cols],
                                                 ACT.Gelu, bias=b1c[:, e * HB + hb:e * HB + hb + 1]
                                                 ).then_inc(gelu_done, 1)
                            k += 1

        @block.vector
        def _(v):
            steps = Steps(v, dve)
            do = steps.mark
            do(v.memset(lneps1[:], LN1_EPS))
            do(v.memset(lneps2[:], LN2_EPS))

            def chain(ins):
                steps.wait(do(ins))

            v.wait_ge(lw_exp, 1)
            chain(v.tensor_scalar(osg[:], sg[:], 1.0, None, ALU.add))
            chain(v.reciprocal(sg[:], osg[:]))
            chain(v.tensor_scalar(osg[:], sg[:], -1.0, 1.0, ALU.mult, ALU.add))
            v.wait_ge(w_in, 16 * 7)
            v.tensor_tensor(bsg[:], bp_c[:], sg[:, 4:5], ALU.mult).then_inc(sg_ready, 1)

            def norm_stats(phase, g):
                for k in range(R * g, R * g + R):
                    last = do(v.bn_stats(stats[:, k, :], X[:, k, :]))
                steps.wait(last)
                s = stats[:, R * g:R * g + R, :].rearrange("p n s -> p s n")
                l = ln[:, phase, :, R * g:R * g + R]
                a = do(v.tensor_tensor(l[:, 1, :], s[:, 1, :], s[:, 4, :], ALU.subtract))
                b = do(v.tensor_tensor(l[:, 0, :], s[:, 1, :], s[:, 4, :], ALU.add))
                c = do(v.tensor_tensor(l[:, 2, :], s[:, 2, :], s[:, 5, :], ALU.add))
                steps.wait(c)
                d = do(v.tensor_tensor(l[:, 1, :], l[:, 1, :], l[:, 1, :], ALU.mult))
                chain(v.tensor_scalar(l[:, 0, :], l[:, 0, :], 0.5, None, ALU.mult))
                v.scalar_tensor_tensor(l[:, 3, :], l[:, 1, :], C / 4.0, l[:, 2, :], ALU.mult,
                                       ALU.add).then_inc(var_ready, 1)

            def norm_spread(phase, g):
                l = ln[:, phase, :, R * g:R * g + R]
                v.wait_ge(std_ready, norm_rank[phase, g] + 1)
                v.reciprocal(l[:, 5, :], l[:, 4, :]).then_inc(rstd_ready, 1)

            def add_residual(g):
                v.wait_ge(osp_turned, g + 1)
                rows = X[:, R * g:R * g + R, :].rearrange("p n c -> p (n c)")
                v.wait_ge(xn_ready, norm_rank[0, g] + 1)
                v.tensor_tensor(rows, PS[:, PERM_BANK, :].bitcast(BF16)[:, 0:W], rows,
                                ALU.add).then_inc(res_added, 1)
                v.wait_ge(res_added, g + 1)

            v.wait_ge(w_ready, 1)
            WpT = wT[:, 3, :]
            chain(v.tensor_copy(wpT[:, 0, :], WpT))
            chain(v.tensor_tensor(wres[:, 0, :], WpT, wpT[:, 0, :], ALU.subtract))
            chain(v.tensor_copy(wpT[:, 1, :], wres[:, 0, :]))
            chain(v.tensor_tensor(wres[:, 1, :], wres[:, 0, :], wpT[:, 1, :], ALU.subtract))
            m = do(v.tensor_copy(wpT[:, 2, :], wres[:, 1, :]))
            steps.wait(m)
            do(v.memset(OM[:], 1.0))
            do(v.memset(U[:], 0.0))
            steps.wait(steps.count)
            for w, col in enumerate((0, 1, 2, 4)):
                do(v.tensor_scalar(OM[:, w, :], OM[:, w, :], osg[:, col:col + 1], None, ALU.mult))
            v.memset(VY[:], 0.0).then_inc(wp_split, 1)
            steps.wait(steps.count)

            def mask_kv(i):
                v.wait_ge(kv_done, i + 1)
                if i >= 2:
                    v.wait_ge(y_done, 2 * i - 2)
                src = PS[:, KV_BANK:KV_BANK + 2, :].rearrange("p h (i c) -> p h i c", i=4)
                dst = KV[i % 2][:].rearrange("p i h c -> p h i c")
                mb = mask[:].rearrange("p h d -> p (h d)").unsqueeze(1).to_broadcast([128, 8, 128])
                mb = mb.rearrange("p (h i) c -> p h i c", h=2)
                v.tensor_tensor(dst, src, mb, ALU.mult).then_inc(kv_masked, 1)

            def y_lif(t):
                v.wait_ge(perm_copied, len(PERM) * (t + 1))
                if t >= 2:
                    v.wait_ge(ring_done, item_rank["qkv", 3, BT * (t - 1) - 1, 0] + 1)
                flat = lambda a: a[:].rearrange("p n b -> p (n b)")
                chain(v.scalar_tensor_tensor(flat(HY), flat(VY), osg[:, 3:4], flat(HY), ALU.mult, ALU.add))
                v.tensor_scalar(ysp[t % 2][:].rearrange("p b n -> p n b"), HY[:], 1.0, None,
                                ALU.is_ge).then_inc(ysp_ready, 1)
                v.scalar_tensor_tensor(flat(VY), flat(HY), 1.0, flat(HY), ALU.is_lt, ALU.mult).then_inc(hy_used, 1)
                v.wait_ge(hy_used, t + 1)

            v.wait_ge(consts, NCONST)
            for slot in range(-1, END):
                if 0 <= slot < SLOTS:
                    lo = 0 if slot < BLOCKS else 3
                    hi = 4 if slot >= LAG else 3
                    h, cur = H[slot % 3], slice(lo, hi)
                    last = ("qkv", 3, slot - LAG, 0) if slot >= LAG else ("qkv", 2, slot, 0)
                    v.wait_ge(ring_copied, item_rank[last] + 1)
                    for st in range(SB):
                        flat = lambda a: a.rearrange("p w n -> p (w n)")
                        m = do(v.tensor_tensor(flat(h[:, st, cur, :]), flat(U[:, cur, :]), flat(h[:, st, cur, :]),
                                               ALU.add))
                        if st == 3 and 1 <= slot <= BLOCKS:
                            mask_kv(slot - 1)
                        steps.wait(m)
                        m = do(v.scalar_tensor_tensor(flat(VV[:, cur, :]), flat(h[:, st, cur, :]), 1.0,
                                                      flat(h[:, st, cur, :]), ALU.is_lt, ALU.mult))
                        steps.wait(m)
                        m = do(v.tensor_tensor(flat(U[:, cur, :]), flat(VV[:, cur, :]), flat(OM[:, cur, :]), ALU.mult))
                        if st == 5:
                            if slot % BT == 1 and 0 < slot // BT <= T:
                                y_lif(slot // BT - 1)
                        steps.wait(m)
                    if slot < BLOCKS:
                        if slot >= 2:
                            v.wait_ge(y_done, 2 * (slot - 1))
                        out_s = spikes[slot % 2][:, :, :, 0:N]
                        m = v.tensor_scalar(out_s, h[:, :, 0:3, :].rearrange("p s w n -> p w s n"), 1.0, None,
                                            ALU.is_ge)
                        m.then_inc(block_done, 1)
                    if slot >= LAG:
                        ob = slot - LAG
                        m = v.tensor_scalar(osp[:, BC * ob:BC * ob + BC].rearrange("p (s n) -> p s n", n=N),
                                            h[:, :, 3, :], 1.0, None, ALU.is_ge)
                        m.then_inc(osp_ready, 1)
                        if slot >= BLOCKS:
                            v.wait_ge(osp_ready, ob + 1)
                            v.sem_inc(block_done, 1)
                for phase, g in norms(slot):
                    if phase == 0:
                        v.wait_ge(x_ready, g + 1)
                    else:
                        add_residual(g)
                    norm_stats(phase, g)
                for x_ in norms(slot):
                    norm_spread(*x_)

            bc = lambda a: a.unsqueeze(2).to_broadcast([128, TILES, E])
            v.wait_ge(logits_done, 1)
            lg = PS[:, 0, 0:TILES * E].rearrange("p (n e) -> p n e", e=E)
            rk = rank[:].unsqueeze(1).to_broadcast([128, TILES, E])
            chain(v.tensor_reduce(g1[:, 0, :], lg, AX.X, ALU.max))
            v.tensor_tensor(gt[:, 0], lg, bc(g1[:, 0, :]), ALU.subtract).then_inc(gate_in, 1)
            v.wait_ge(gate_exp, 1)
            ex = gt[:, 1]
            chain(v.tensor_reduce(g1[:, 1, :], ex, AX.X, ALU.add))

            def first_largest(src, m, hit):
                chain(v.tensor_reduce(m, src, AX.X, ALU.max))
                chain(v.tensor_tensor(gt[:, 2], src, bc(m), ALU.is_equal))
                chain(v.tensor_tensor(gt[:, 2], gt[:, 2], rk, ALU.mult))
                chain(v.tensor_reduce(g1[:, 5, :], gt[:, 2], AX.X, ALU.max))
                chain(v.tensor_tensor(hit, gt[:, 2], bc(g1[:, 5, :]), ALU.is_equal))

            first_largest(ex, g1[:, 2, :], gt[:, 3])
            chain(v.scalar_tensor_tensor(gt[:, 4], gt[:, 3], -2.0, ex, ALU.mult, ALU.add))
            first_largest(gt[:, 4], g1[:, 3, :], gt[:, 5])
            chain(v.tensor_tensor(g1[:, 2, :], g1[:, 2, :], g1[:, 3, :], ALU.add))
            chain(v.scalar_tensor_tensor(g1[:, 2, :], g1[:, 1, :], GATE_EPS, g1[:, 2, :], ALU.mult, ALU.add))
            chain(v.reciprocal(g1[:, 4, :], g1[:, 2, :]))
            chain(v.tensor_tensor(gt[:, 3], gt[:, 3], gt[:, 5], ALU.add))
            chain(v.tensor_tensor(gt[:, 4], gt[:, 3], ex, ALU.mult))
            chain(v.tensor_tensor(score[:], gt[:, 4], bc(g1[:, 4, :]), ALU.mult))
            v.wait_ge(ffn_in, 16 * 4)
            v.wait_ge(w_turned, 2)
            v.tensor_copy(b1c[:], PS[:, 1, 0:E * HB]).then_inc(score_ready, 1)
            v.wait_ge(xn_ready, 2 * G)

            k = 0
            for g in range(G):
                for c0, c1 in CUTS:
                    for e in range(E):
                        v.wait_ge(down_done, k + 1)
                        for c in range(c1 - c0):
                            n = R * g + c0 + c
                            sc = score[:, n, e:e + 1]
                            m = do(v.scalar_tensor_tensor(XD2[:, k % 2, c, :], b2b[:, e, :], sc, X[:, n, :],
                                                          ALU.mult, ALU.add))
                        steps.wait(m)
                        for c in range(c1 - c0):
                            n = R * g + c0 + c
                            sc = score[:, n, e:e + 1]
                            m = do(v.scalar_tensor_tensor(X[:, n, :], PS[:, 4 + k % 2, c * 128:c * 128 + 128], sc,
                                                          XD2[:, k % 2, c, :], ALU.mult, ALU.add))
                        steps.wait(m)
                        v.sem_inc(y_added, 1)
                        k += 1
                v.sem_inc(out_ready, 1)

        @block.tensor
        def _(pe):
            pe.wait_ge(consts, NCONST)
            pe.wait_ge(w_in, 16 * 7)
            for i in range(4):
                m = pe.transpose(PS[:, 0, i * 128:i * 128 + 128], wrow[:, i, :], identf[:])
            m.then_inc(w_turned, 1)
            pe.wait_ge(w_ready, 1)

            def ring_item(item):
                kind, w, b, c = item
                n = item_rank[item]
                bank = PS[:, RING + n % 2, :]
                if n >= 2:
                    pe.wait_ge(ring_copied, n - 1)
                if kind == "turn":
                    k0, k1 = CUTS[c]
                    pe.wait_ge(xn_ready, norm_rank[w, b] + 1)
                    for r in range(k0, k1):
                        m = pe.transpose(bank[:, (r - k0) * 128:(r - k0) * 128 + 128], XN[:, r, :], identf[:])
                    m.then_inc(ring_done, 1)
                    if c:
                        pe.wait_ge(ring_done, n + 1)
                        pe.sem_inc(xt_turned, 1)
                elif w < 3:
                    g = (BC * (b + 1) - 1) // W
                    pe.wait_ge(ring_copied, item_rank["turn", 0, g, 1] + 1)
                    pe.matmul(bank[:, 0:BC], wT[:, w, :], xT[:, BC * b:BC * b + BC], start=True,
                              stop=True).then_inc(ring_done, 1)
                else:
                    t = b // BT
                    pe.wait_ge(ysp_ready, t + 1)
                    src = ysp[t % 2][:, SB * (b % BT):SB * (b % BT) + SB, :].rearrange("p b n -> p (b n)")
                    for part in range(3):
                        m = pe.matmul(bank[:, 0:BC], wpT[:, part, :], src, start=(part == 0), stop=(part == 2))
                    m.then_inc(ring_done, 1)

            def pair(w, p):
                p *= 2
                return spikes[p // SB % 2][:, w, p % SB:p % SB + 2, :].rearrange("p h n -> p (h n)")

            def turn_kv(i):
                pe.wait_ge(block_done, i + 1)
                if i:
                    pe.wait_ge(kvt_copied, i)
                bank = PS[:, KVT_BANK, :].bitcast(BF16)
                for w in range(2):
                    for a in range(4):
                        k = (w * 4 + a) * 128
                        m = pe.transpose(bank[:, k:k + 128], pair(1 + w, 4 * i + a), identb[:])
                m.then_inc(kvt_turned, 1)

            def key_value(i):
                pe.wait_ge(kvt_copied, i + 1)
                if i:
                    pe.wait_ge(kv_masked, i)
                for a in range(4):
                    for par in range(2):
                        rows = slice(64 * par, 64 * par + N)
                        m = pe.matmul(PS[:, KV_BANK + par, a * 128:a * 128 + 128], KVT[i % 2][rows, 0, a, :],
                                      KVT[i % 2][rows, 1, a, :], start=True, stop=True)
                m.then_inc(kv_done, 1)

            def query(i):
                pe.wait_ge(kv_masked, i + 1)
                for half in range(2):
                    if i:
                        pe.wait_ge(y_copied, 4 * (i - 1) + 2 * half + 2)
                    for a in range(2):
                        m = pe.matmul(PS[:, Y_BANK + half, a * 256:a * 256 + 256], pair(0, 4 * i + 2 * half + a),
                                      KV[i % 2][:, 2 * half + a, :, :].rearrange("p h c -> p (h c)"), start=True,
                                      stop=True)
                    m.then_inc(y_done, 1)

            perm_bank_users = [0, 0]

            def permute(t):
                pe.wait_ge(y_copied, 4 * BT * (t + 1))
                if perm_bank_users[1]:
                    pe.wait_ge(res_added, perm_bank_users[1])
                for n0, n1 in PERM:
                    if perm_bank_users[0]:
                        pe.wait_ge(perm_copied, perm_bank_users[0])
                    perm_bank_users[0] += 1
                    for n in range(n0, n1):
                        chans = range(128 * n // N, (128 * n + 127) // N + 1)
                        for par in range(2):
                            col = ((n - n0) * 2 + par) * (B // 2)
                            for ch in chans:
                                s = N * ch - 128 * n
                                m = pe.matmul(PS[:, PERM_BANK, col:col + B // 2],
                                              shift[:, par, 127 - s:255 - s],
                                              Y[:, ch, t * B // 2:(t + 1) * B // 2], start=(ch == chans[0]),
                                              stop=(ch == chans[-1]))
                    m.then_inc(perm_done, 1)

            def turn_out(g):
                pe.wait_ge(osp_ready, norm2_block(g) + 1)
                if perm_bank_users[0]:
                    pe.wait_ge(perm_copied, perm_bank_users[0])
                if perm_bank_users[1]:
                    pe.wait_ge(res_added, perm_bank_users[1])
                perm_bank_users[1] += 1
                for r in range(R):
                    k = R * g + r
                    m = pe.transpose(PS[:, PERM_BANK, :].bitcast(BF16)[:, r * 128:r * 128 + 128],
                                     osp[:, k * 128:k * 128 + 128], identb[:])
                m.then_inc(osp_turned, 1)

            pe.wait_ge(wp_split, 1)
            for slot in range(-1, END):
                for phase, g in norms(slot):
                    if phase:
                        turn_out(g)
                for it in ring[slot]:
                    ring_item(it)
                if 1 <= slot <= BLOCKS:
                    turn_kv(slot - 1)
                    key_value(slot - 1)
                    query(slot - 1)
                    if slot % BT == 0:
                        permute(slot // BT - 1)

            pe.wait_ge(ffn_in, 16 * 4)
            pe.wait_ge(ring_copied, len(item_rank))
            pe.transpose(PS[:, 1, 0:E * HB], b1r[:], identf[0:E * HB, 0:E * HB]).then_inc(w_turned, 1)
            for n in range(TILES):
                m = pe.matmul(PS[:, 0, n * E:n * E + E], xT[:, n * 128:n * 128 + 128], Wg_s[:], start=True, stop=True)
            m.then_inc(logits_done, 1)

            def up(k, g, c0, c1, e):
                src = xT[:, 128 * (R * g + c0):128 * (R * g + c1)]
                for hb in range(HB):
                    if k:
                        pe.wait_ge(gelu_done, HB * (k - 1) + hb + 1)
                    pe.matmul(PS[:, hb, 0:128 * (c1 - c0)], W1_s[:, e, hb * 128:hb * 128 + 128], src, start=True,
                              stop=True).then_inc(up_done, 1)

            def down(k, g, c0, c1, e):
                pe.wait_ge(gelu_done, HB * (k + 1))
                if k >= 2:
                    pe.wait_ge(y_added, k - 1)
                for c in range(c1 - c0):
                    for hb in range(HB):
                        m = pe.matmul(PS[:, 4 + k % 2, c * 128:c * 128 + 128],
                                      hid[k % 2][:, hb, c * 128:c * 128 + 128], W2_s[:, e, hb, :],
                                      start=(hb == 0), stop=(hb == HB - 1))
                m.then_inc(down_done, 1)

            pe.wait_ge(score_ready, 1)
            items = [(g, c0, c1, e) for g in range(G) for c0, c1 in CUTS for e in range(E)]
            for k, it in enumerate(items):
                up(k, *it)
                if k:
                    down(k - 1, *items[k - 1])
            down(len(items) - 1, *items[-1])


_INS = ["x", "L0_conv_Wq", "L0_conv_Wk", "L0_conv_Wv", "L0_conv_Wp", "L0_conv_bp", "lif_w", "L0_ffn_Wg",
        "L0_ffn_W1", "L0_ffn_b1", "L0_ffn_W2", "L0_ffn_b2"]


def kernel(**inputs):
    import numpy as np
    import concourse.bacc as bacc
    from concourse import mybir as mb
    from concourse.bass_utils import run_bass_kernel_spmd

    lifs = [np.reshape(inputs[f"L0_conv_{n}"], (1,)) for n in ("wq", "wk", "wv", "wa", "wp")]
    inputs = {**inputs, "lif_w": np.concatenate(lifs)}
    nc = bacc.Bacc("TRN2", target_bir_lowering=False, num_devices=1)
    arrays, args = {}, []
    for name in _INS:
        a = np.ascontiguousarray(inputs[name])
        arrays[f"in_{name}"] = a
        args.append(nc.dram_tensor(f"in_{name}", a.shape, mb.dt.from_np(a.dtype), kind="ExternalInput").ap())
    out = nc.dram_tensor("out", inputs["x"].shape, mb.dt.float32, kind="ExternalOutput").ap()
    metaformer_block(nc, *args, out)
    r = run_bass_kernel_spmd(nc, [arrays], core_ids=[0])
    return r.results[0]["out"]
```

```python
from contextlib import ExitStack

import concourse.bass as bass
from concourse import mybir

ALU = mybir.AluOpType
ACT = mybir.ActivationFunctionType
AX = mybir.AxisListType
F32 = mybir.dt.float32
BF16 = mybir.dt.bfloat16
I32 = mybir.dt.int32
F16 = mybir.dt.float16


class Steps:

    def __init__(self, engine, semaphore):
        self.engine, self.semaphore, self.base, self.count = engine, semaphore, 0, 0

    def mark(self, instruction):
        instruction.then_inc(self.semaphore, 1)
        self.count += 1
        return self.count

    def wait(self, mark):
        self.engine.wait_ge(self.semaphore, self.base + mark)


def metaformer_block(nc, x, Wq, Wk, Wv, Wp, bp, lif_w, Wg, W1, b1, W2, b2, out):
    T, B, N, C = x.shape
    TB = T * B
    E, _, HID = W1.shape
    HB = HID // 128
    HEADS = 8
    D = C // HEADS
    NPAD = 64
    PAIRS = TB // 2
    LN1_EPS, LN2_EPS, GATE_EPS = 1e-6, 1e-5, 1e-6
    TOK = TB * N
    TILES = TOK // 128
    R = 7
    G = TILES // R
    SB = 8
    BLOCKS = TB // SB
    BC = SB * N
    LAG = 7
    SLOTS = BLOCKS + LAG
    assert C == 128 and TB == 128 and HID % 128 == 0 and TOK % (128 * R) == 0 and N <= NPAD and BC <= 512
    W = R * 128
    CUTS = [(0, 4), (4, R)]
    BT = BLOCKS // T
    ROWS = 256
    HALVES = ROWS // 128
    CAP = TOK + ROWS
    PIECES = 2 * TOK // ROWS + E - 1
    PIECES += -PIECES % 4
    PAYLOAD = C + 2
    SKIPPED = 2.0 ** 20
    COUNTS = -(-TOK // ROWS)
    assert 2 * TOK % ROWS == 0
    AHEAD = 2
    DEEP = 4
    assert PIECES % DEEP == 0

    x_v = x.rearrange("t b n c -> (t b n) c").rearrange("(k p) c -> p k c", p=128)
    out_v = out.rearrange("t b n c -> (t b n) c").rearrange("(k p) c -> p k c", p=128)

    def norm1_block(g):
        return W * g // BC

    def norm2_block(g):
        return (W * (g + 1) - 1) // BC

    norm1_slot = {g: norm1_block(g) - 3 for g in range(G)}
    norm2_slot = {g: norm2_block(g) + LAG + 1 for g in range(G)}
    END = max(norm2_slot.values()) + 4

    def gate_group(slot, behind):
        return [g for g in range(G) if norm2_slot[g] + behind == slot]

    def ring_items(slot):
        got = []
        for g in range(G):
            if (norm1_slot[g] + 1 if norm1_slot[g] > -1 else -1) == slot:
                got += [("turn", 0, g, c) for c in range(2)]
        if slot + 1 < BLOCKS:
            got += [("qkv", w, slot + 1, 0) for w in range(3)]
        if 0 <= slot + 1 - LAG < BLOCKS:
            got.append(("qkv", 3, slot + 1 - LAG, 0))
        for g in gate_group(slot, 1):
            got += [("turn", 1, g, c) for c in range(2)]
        return got

    def norms(slot):
        return ([(0, g) for g in range(G) if max(norm1_slot[g], -1) == slot]
                + [(1, g) for g in range(G) if norm2_slot[g] == slot])

    norm_order = [x for s in range(-1, END) for x in norms(s)]
    norm_rank = {x: i for i, x in enumerate(norm_order)}
    item_rank, ring = {}, {}
    for s in range(-1, END):
        ring[s] = ring_items(s)
        for it in ring[s]:
            item_rank[it] = len(item_rank)

    ctx = ExitStack()
    with ctx:
        def sb(name, shape, dt=F32):
            return ctx.enter_context(nc.sbuf_tensor(name, shape, dt))

        def sem(name):
            return ctx.enter_context(nc.semaphore(name))

        PS = ctx.enter_context(nc.psum_tensor("PS", [128, 8, 512], F32))
        RING, KVT_BANK, KV_BANK, Y_BANK, GATE_BANK, PERM_BANK = 0, 2, 3, 5, 6, 7

        X = sb("X", [128, TILES, C])
        XD = sb("XD", [128, R, C])
        XN = sb("XN", [128, R, C])
        xT = sb("xT", [128, TOK])
        spikes = [sb(f"spikes{i}", [128, 3, SB, NPAD], BF16) for i in range(2)]
        H = [sb(f"H{i}", [128, SB, 4, N]) for i in range(3)]
        U = sb("U", [128, 4, N])
        VV = sb("VV", [128, 4, N])
        OM = sb("OM", [128, 4, N])
        KVT = [sb(f"KVT{i}", [128, 2, 4, 128], BF16) for i in range(2)]
        KV = [sb(f"KV{i}", [128, 4, 2, 128], BF16) for i in range(2)]
        Y = sb("Y", [128, C, PAIRS], F16)
        HY = sb("HY", [128, N, B])
        VY = sb("VY", [128, N, B])
        ysp = [sb(f"ysp{i}", [128, B, N], BF16) for i in range(2)]
        osp = sb("osp", [128, TOK], BF16)
        shift = sb("shift", [128, 2, 304], F16)
        mask = sb("mask", [128, HEADS, D])
        identf = sb("identf", [128, 128])
        identb = sb("identb", [128, 128], BF16)
        ones = HY[:].rearrange("p n b -> p (n b)")[:, 0:608].rearrange("p (a b) -> p a b", a=2)
        wrow = HY[:].rearrange("p n b -> p (n b)")[:, 608:1120].rearrange("p (a b) -> p a b", a=4)
        wT = sb("wT", [128, 4, C])
        wpT = sb("wpT", [128, 3, C], BF16)
        wres = VY[:].rearrange("p n b -> p (n b)")[:, 0:2 * C].rearrange("p (a b) -> p a b", a=2)
        bp_c = sb("bp_c", [128, 1])
        bsg = sb("bsg", [128, 1])
        lw = sb("lw", [128, 5])
        sg = sb("sg", [128, 5])
        osg = sb("osg", [128, 5])
        stats = sb("stats", [128, TILES, 6])
        ln = sb("ln", [128, 2, 6, TILES])
        Wg_s = sb("Wg_s", [128, E])
        W1_s = sb("W1_s", [128, E, HID])
        W2_s = sb("W2_s", [128, E, HB, C])
        b1r = sb("b1r", [E * HB, 128])
        b1c = sb("b1c", [128, E * HB])
        b2b = sb("b2b", [128, E, C])
        rank = sb("rank", [128, E])
        score = sb("score", [128, TILES, 2])
        XG = [sb(f"XG{i}", [128, R, PAYLOAD]) for i in range(2)]
        pad_rows = sb("pad_rows", [128, HALVES, PAYLOAD])
        twice_token = sb("twice_token", [128, TILES])
        gate = sb("gate", [128, 7, R, E])
        gate1 = sb("gate1", [128, 6, R])
        chosen = sb("chosen", [128, R + 1, E], BF16)
        before = sb("before", [128, 128], BF16)
        all_ones = sb("all_ones", [128, 128], BF16)
        filled = sb("filled", [128, E])
        place = [sb(f"place{i}", [128, 2, R], I32) for i in range(2)]
        upto = sb("upto", [128, E, E])
        region = sb("region", [128, E])
        counts_at = sb("counts_at", [128, COUNTS])
        piece_no = sb("piece_no", [128, PIECES])
        tally = sb("tally", [128, E, COUNTS])
        passed = sb("passed", [128, 2, PIECES, E])
        count1 = sb("count1", [128, 5, E])
        piece_rank = sb("piece_rank", [128, PIECES])
        piece_f = sb("piece_f", [128, 2, PIECES])
        piece_expert = sb("piece_expert", [128, PIECES], I32)
        piece_start = sb("piece_start", [128, PIECES], I32)
        region_end = sb("region_end", [128, E], I32)
        rows_in = [sb(f"rows_in{i}", [128, HALVES, PAYLOAD]) for i in range(DEEP)]
        rows_T = [sb(f"rows_T{i}", [128, ROWS]) for i in range(2)]
        target = [sb(f"target{i}", [128, HALVES], I32) for i in range(DEEP)]
        b1_now = [sb(f"b1_now{i}", [128, HB]) for i in range(2)]
        lneps1 = sb("lneps1", [128, 1])
        lneps2 = sb("lneps2", [128, 1])
        free = Y[:].rearrange("p c n -> p (c n)").bitcast(F32)
        hid = [free[:, i * HB * ROWS:(i + 1) * HB * ROWS].rearrange("p (b c) -> p b c", b=HB) for i in range(2)]
        w_now = [free[:, (2 + i) * HB * ROWS:(3 + i) * HB * ROWS].rearrange("p (l c) -> p l c", l=2)
                 for i in range(2)]
        rows_out = [osp[:].bitcast(F32)[:, i * ROWS:(i + 1) * ROWS].rearrange("p (a c) -> p a c", a=HALVES)
                    for i in range(DEEP)]
        shares = ([xT[:, i * 2 * W:(i + 1) * 2 * W] for i in range(3)]
                  + [W1_s[:].rearrange("p e h -> p (e h)")[:, i * 2 * W:(i + 1) * 2 * W] for i in range(2)]
                  + [W2_s[:].rearrange("p e b c -> p (e b c)")[:, i * 2 * W:(i + 1) * 2 * W] for i in range(2)])
        shares = [a.rearrange("p (n k c) -> p n k c", k=2, c=C) for a in shares]
        by_expert = nc.dram_tensor("by_expert", (E * CAP + ROWS, PAYLOAD), F32, kind="Internal").ap()
        by_token = nc.dram_tensor("by_token", (2 * TOK, C), F32, kind="Internal").ap()
        by_token_v = by_token.rearrange("(n p k) c -> p n k c", p=128, k=2)

        x_in = [sem(f"x_in{g}") for g in range(G)]
        x_ready = sem("x_ready")
        w_in = sem("w_in")
        ffn_in = sem("ffn_in")
        consts = sem("consts")
        dve = sem("dve_step")
        actst = sem("act_step")
        pools = sem("pool_step")
        lw_exp = sem("lw_exp")
        sg_ready = sem("sg_ready")
        w_turned = sem("w_turned")
        w_ready = sem("w_ready")
        wp_split = sem("wp_split")
        var_ready = sem("var_ready")
        std_ready = sem("std_ready")
        rstd_ready = sem("rstd_ready")
        xn_ready = sem("xn_ready")
        xt_turned = sem("xt_turned")
        ring_done = sem("ring_done")
        ring_copied = sem("ring_copied")
        block_done = sem("block_done")
        kvt_turned = sem("kvt_turned")
        kvt_copied = sem("kvt_copied")
        kv_done = sem("kv_done")
        kv_masked = sem("kv_masked")
        y_done = sem("y_done")
        y_copied = sem("y_copied")
        perm_done = sem("perm_done")
        perm_copied = sem("perm_copied")
        hy_used = sem("hy_used")
        ysp_ready = sem("ysp_ready")
        osp_ready = sem("osp_ready")
        osp_turned = sem("osp_turned")
        res_added = sem("res_added")
        logits_done = sem("logits_done")
        gate_in = sem("gate_in")
        gate_exp = sem("gate_exp")
        logits_used = sem("logits_used")
        chosen_ready = sem("chosen_ready")
        ranked = sem("ranked")
        place_ready = sem("place_ready")
        scattered = [sem(f"scattered{i}") for i in range(2)]
        pieces_ready = sem("pieces_ready")
        padded = sem("padded")
        piece_in = [sem(f"piece_in{i}") for i in range(DEEP)]
        piece_read = sem("piece_read")
        piece_turned = sem("piece_turned")
        piece_copied = sem("piece_copied")
        w1_set = sem("w1_set")
        w2_set = sem("w2_set")
        b1_set = sem("b1_set")
        up_done = sem("up_done")
        gelu_done = sem("gelu_done")
        down_done = sem("down_done")
        rows_ready = sem("rows_ready")
        rows_taken = sem("rows_taken")
        rows_sent = [sem(f"rows_sent{i}") for i in range(DEEP)]
        shares_in = [sem(f"shares_in{g}") for g in range(G)]
        out_ready = sem("out_ready")
        stored = sem("stored")

        block = ctx.enter_context(nc.Block())
        PERM = [(n, min(n + 14, N)) for n in range(0, N, 14)]

        @block.sync
        def _(sp):
            for g in range(G):
                sp.dma_start(X[:, R * g:R * g + R, :], x_v[:, R * g:R * g + R, :]).then_inc(x_in[g], 16)
            sp.dma_start(W1_s[:], W1.rearrange("e c h -> c e h")).then_inc(ffn_in, 16)
            sp.dma_start(W2_s[:], W2.rearrange("e (b h) c -> h e b c", h=128)).then_inc(ffn_in, 16)
            sp.dma_start(b1r[:], b1.rearrange("e (b h) -> (e b) h", h=128)).then_inc(ffn_in, 16)
            sp.dma_start(b2b[:], b2.rearrange("e c -> (e c)").partition_broadcast(128)
                         .rearrange("p (e c) -> p e c", c=C)).then_inc(ffn_in, 16)
            for g in range(G):
                sp.wait_ge(x_in[g], 16)
                sp.sem_inc(x_ready, 1)
            sp.wait_ge(pieces_ready, 1)
            pad_src = pad_rows[:]
            for e in range(E):
                end = sp.value_load(region_end[0:1, e:e + 1], min_val=e * CAP, max_val=e * CAP + TOK)
                sp.dma_start(by_expert[bass.ds(end, ROWS), :].rearrange("(p a) c -> p a c", a=HALVES),
                             pad_src).then_inc(padded, 16)
            sp.dma_start(by_expert[E * CAP:E * CAP + ROWS, :].rearrange("(p a) c -> p a c", a=HALVES),
                         pad_src).then_inc(padded, 16)
            sp.wait_ge(padded, 16 * (E + 1))
            for i in range(2):
                sp.wait_ge(scattered[i], 16 * 2 * R * ((G + 1 - i) // 2))
            with sp.Fori(0, PIECES // DEEP) as i:
                for b in range(DEEP):
                    start = sp.value_load(piece_start[0:1, bass.ds(DEEP * i + b, 1)], min_val=0, max_val=E * CAP)
                    sp.wait_ge(piece_read, DEEP * i + b + 1)
                    sp.dma_start(rows_in[b][:], by_expert[bass.ds(start, ROWS), :]
                                 .rearrange("(p a) c -> p a c", a=HALVES)).then_inc(piece_in[b], 16)
            for b in range(DEEP):
                sp.wait_ge(rows_sent[b], 16 * HALVES * (PIECES // DEEP))
            sp.wait_ge(down_done, PIECES + AHEAD)
            for g in range(G):
                sp.dma_start(shares[g], by_token_v[:, R * g:R * g + R]).then_inc(shares_in[g], 16)
            for g in range(G):
                sp.wait_ge(out_ready, g + 1)
                sp.dma_start(out_v[:, R * g:R * g + R, :], X[:, R * g:R * g + R, :]).then_inc(stored, 16)
            sp.wait_ge(stored, 16 * G)

        @block.gpsimd
        def _(pool):
            steps = Steps(pool, pools)
            steps.mark(pool.memset(ones, 1.0))
            steps.mark(pool.memset(spikes[0][:, :, :, N:NPAD], 0.0))
            steps.mark(pool.memset(spikes[1][:, :, :, N:NPAD], 0.0))
            pool.memset(Y[:], 0.0).then_inc(consts, 1)
            steps.wait(3)
            one = ones[:, 0, 0:128]
            pool.affine_select(out=identf[:], in_=one, compare_op=ALU.is_equal, fill=0.0, base=0,
                               pattern=[[-1, 128]], channel_multiplier=1).then_inc(consts, 1)
            pool.affine_select(out=identb[:], in_=one, compare_op=ALU.is_equal, fill=0.0, base=0,
                               pattern=[[-1, 128]], channel_multiplier=1).then_inc(consts, 1)
            pool.affine_select(out=shift[:], in_=ones, compare_op=ALU.is_equal, fill=0.0, base=127,
                               pattern=[[-64, 2], [-1, 304]], channel_multiplier=1).then_inc(pools, 1)
            steps.count += 1
            steps.wait(steps.count)
            pool.memset(shift[64:128, 0, :], 0.0).then_inc(consts, 1)
            pool.memset(shift[0:64, 1, :], 0.0).then_inc(consts, 1)
            pool.wait_ge(consts, 5)
            m1 = pool.affine_select(out=mask[:], in_=ones[:, 0, 0:128].rearrange("p (h d) -> p h d", d=D),
                                    compare_op=ALU.is_ge, fill=0.0, base=0,
                                    pattern=[[-D, HEADS], [0, D]], channel_multiplier=1)
            m = steps.mark(m1)
            steps.wait(m)
            pool.affine_select(out=mask[:], in_=mask[:], compare_op=ALU.is_ge, fill=0.0, base=D - 1,
                               pattern=[[D, HEADS], [0, D]], channel_multiplier=-1).then_inc(consts, 1)
            pool.iota(rank[:], pattern=[[-1, E]], base=E, channel_multiplier=0,
                      allow_small_or_imprecise_dtypes=True).then_inc(consts, 1)
            pool.memset(all_ones[:], 1.0).then_inc(consts, 1)
            pool.affine_select(out=before[:], in_=one, compare_op=ALU.is_ge, fill=0.0, base=-1,
                               pattern=[[1, 128]], channel_multiplier=-1).then_inc(consts, 1)
            pool.affine_select(out=upto[:], in_=ones[:, 0, 0:E * E].rearrange("p (e f) -> p e f", f=E),
                               compare_op=ALU.is_ge, fill=0.0, base=0, pattern=[[1, E], [-1, E]],
                               channel_multiplier=0).then_inc(consts, 1)
            for table, pattern, channel in ((twice_token, [[256, TILES]], 2), (region, [[CAP, E]], 0),
                                            (counts_at, [[ROWS, COUNTS]], 0), (piece_no, [[1, PIECES]], 0)):
                pool.iota(table[:], pattern=pattern, base=0, channel_multiplier=channel,
                          allow_small_or_imprecise_dtypes=True).then_inc(consts, 1)
            pool.memset(chosen[:], 0.0).then_inc(consts, 1)
            m = steps.mark(pool.memset(pad_rows[:], 0.0))
            steps.wait(m)
            pool.memset(pad_rows[:, :, C:C + 1], SKIPPED).then_inc(consts, 1)

            def normalise(phase, g):
                k = norm_rank[phase, g]
                rows = X[:, R * g:R * g + R, :]
                bc = lambda row: ln[:, phase, row, R * g:R * g + R].unsqueeze(2).to_broadcast([128, R, C])
                pool.wait_ge(rstd_ready, k + 1)
                if k:
                    pool.wait_ge(xn_ready, k)
                m = steps.mark(pool.tensor_tensor(XD[:], rows, bc(0), ALU.subtract))
                steps.wait(m)
                if phase == 0:
                    if g:
                        pool.wait_ge(xt_turned, max(norm_rank[0, g - 1] + 1, 1))
                    dst = XN[:]
                else:
                    if g >= 2:
                        pool.wait_ge(scattered[g % 2], 16 * 2 * R * (g // 2))
                        pool.wait_ge(xt_turned, norm_rank[1, g - 2] + 1)
                    m = steps.mark(pool.tensor_copy(XG[g % 2][:, :, C], twice_token[:, R * g:R * g + R]))
                    steps.wait(m)
                    dst = XG[g % 2][:, :, 0:C]
                pool.tensor_tensor(dst, XD[:], bc(5), ALU.mult).then_inc(xn_ready, 1)

            def scatter(g):
                pool.wait_ge(place_ready, 2 * g + 2)
                pool.wait_ge(xn_ready, norm_rank[1, g] + 1)
                for r in range(R):
                    for k in range(2):
                        pool.indirect_dma_start(by_expert, bass.IndirectOffsetOnAxis(
                            ap=place[g % 2][:, k, r:r + 1], axis=0), XG[g % 2][:, r, :], None).then_inc(scattered[g % 2], 16)

            for slot in range(-1, END):
                for x_ in norms(slot):
                    normalise(*x_)
                for g in gate_group(slot, 3):
                    scatter(g)

            last_row = pool.alloc_register("last_row")
            pool.reg_mov(last_row, 2 * TOK - 1)
            with pool.Fori(0, PIECES // DEEP) as i:
                for b in range(DEEP):
                    pool.wait_ge(piece_read, DEEP * (i + 1) + b + 1)
                    pool.wait_ge(rows_ready, AHEAD + DEEP * i + b + 1)
                    pool.sem_inc(rows_taken, 1)
                    for a in range(HALVES):
                        pool.indirect_dma_start(by_token, bass.IndirectOffsetOnAxis(
                            ap=target[b][:, a:a + 1], axis=0), rows_out[b][:, a, :], None,
                            bounds_check=last_row, oob_is_err=False).then_inc(rows_sent[b], 16)

        NCONST = 16

        @block.scalar
        def _(act):
            with nc.allow_non_contiguous_dma(reason="a column of biases"):
                for i, w in enumerate((Wq, Wk, Wv, Wp)):
                    act.dma_start(wrow[:, i, :], w).then_inc(w_in, 16)
                act.dma_start(lw[:], lif_w.partition_broadcast(128)).then_inc(w_in, 16)
                act.dma_start(bp_c[:], bp.rearrange("(c a) -> c a", a=1)).then_inc(w_in, 16)
                act.dma_start(Wg_s[:], Wg).then_inc(w_in, 16)
            act.wait_ge(w_in, 16 * 7)
            nc.scalar.activation(sg[:], lw[:], ACT.Exp, scale=-1.0).then_inc(lw_exp, 1)
            act.wait_ge(w_turned, 1)
            nc.scalar.activation(wT[:].rearrange("p a c -> p (a c)"), PS[:, 0, :], ACT.Copy).then_inc(w_ready, 1)
            act.wait_ge(sg_ready, 1)

            def spread(phase, g):
                act.wait_ge(var_ready, norm_rank[phase, g] + 1)
                cols = slice(R * g, R * g + R)
                nc.scalar.activation(ln[:, phase, 4, cols], ln[:, phase, 3, cols], ACT.Sqrt,
                                     bias=(lneps1, lneps2)[phase][:], scale=1.0 / C).then_inc(std_ready, 1)

            def copy_item(item):
                kind, w, b, c = item
                n = item_rank[item]
                act.wait_ge(ring_done, n + 1)
                bank = PS[:, RING + n % 2, :]
                if kind == "turn":
                    k0, k1 = (R * b + x for x in CUTS[c])
                    nc.scalar.activation(xT[:, 128 * k0:128 * k1], bank[:, 0:128 * (k1 - k0)],
                                         ACT.Copy).then_inc(ring_copied, 1)
                    return
                slot = b + (LAG if w == 3 else 0)
                if slot >= 3:
                    act.wait_ge(block_done, slot - 2)
                dst = H[slot % 3][:, :, w, :]
                src = bank[:, 0:BC].rearrange("p (s n) -> p s n", n=N)
                if w == 3:
                    nc.scalar.activation(dst, src, ACT.Identity, scale=sg[:, 4:5],
                                         bias=bsg[:, 0:1]).then_inc(ring_copied, 1)
                else:
                    nc.scalar.activation(dst, src, ACT.Copy, scale=sg[:, w:w + 1]).then_inc(ring_copied, 1)

            def copy_kvt(i):
                act.wait_ge(kvt_turned, i + 1)
                if i >= 2:
                    act.wait_ge(kv_done, i - 1)
                nc.scalar.activation(KVT[i % 2][:].rearrange("p w a c -> p (w a c)"), PS[:, KVT_BANK, :].bitcast(BF16),
                                     ACT.Copy).then_inc(kvt_copied, 1)

            def copy_y(i):
                for half in range(2):
                    act.wait_ge(y_done, 2 * i + half + 1)
                    for par in range(2):
                        rows = slice(64 * par, 64 * par + N)
                        src = PS[rows, Y_BANK, :].rearrange("p (i h c) -> p i h c", i=2, h=2)[:, :, par, :]
                        p0 = 4 * i + 2 * half
                        nc.scalar.activation(Y[rows, :, p0:p0 + 2].rearrange("p c i -> p i c"), src,
                                             ACT.Copy, scale=D ** -0.5).then_inc(y_copied, 1)

            def copy_perm(t):
                if t:
                    act.wait_ge(hy_used, t)
                for c, (n0, n1) in enumerate(PERM):
                    act.wait_ge(perm_done, len(PERM) * t + c + 1)
                    k = n1 - n0
                    src = PS[:, PERM_BANK, 0:k * B].rearrange("p (n h j) -> p n h j", n=k, h=2)
                    dst = HY[:, n0:n1, :].rearrange("p n (j h) -> p n h j", h=2)
                    nc.scalar.activation(dst, src, ACT.Copy, scale=sg[:, 3:4]).then_inc(perm_copied, 1)

            def gate_exponents(g):
                act.wait_ge(gate_in, g + 1)
                nc.scalar.activation(gate[:, 1], gate[:, 0], ACT.Exp).then_inc(gate_exp, 1)
                nc.scalar.activation(gate1[:, 2], gate1[:, 1], ACT.Exp).then_inc(gate_exp, 1)

            for slot in range(-1, END):
                if slot < 0:
                    for x_ in norms(slot):
                        spread(*x_)
                for it in ring[slot]:
                    copy_item(it)
                if 1 <= slot <= BLOCKS:
                    copy_kvt(slot - 1)
                    copy_y(slot - 1)
                    if slot % BT == 0:
                        copy_perm(slot // BT - 1)
                if slot >= 0:
                    for x_ in norms(slot):
                        spread(*x_)
                for g in gate_group(slot, 2):
                    gate_exponents(g)

            def gelu(j, b):
                act.wait_ge(down_done, j + 1)
                act.wait_ge(b1_set, j + 1)
                for hb in range(HB):
                    act.wait_ge(up_done, HB * (j + AHEAD) + hb + 1)
                    nc.scalar.activation(hid[b][:, hb, :], PS[:, hb, 0:ROWS], ACT.Gelu,
                                         bias=b1_now[b][:, hb:hb + 1]).then_inc(gelu_done, 1)

            with act.Fori(0, PIECES // DEEP) as i:
                for b in range(DEEP):
                    gelu(DEEP * i + b, b % 2)

        @block.vector
        def _(v):
            steps = Steps(v, dve)
            do = steps.mark
            do(v.memset(lneps1[:], LN1_EPS))
            do(v.memset(lneps2[:], LN2_EPS))

            def chain(ins):
                steps.wait(do(ins))

            v.wait_ge(lw_exp, 1)
            chain(v.tensor_scalar(osg[:], sg[:], 1.0, None, ALU.add))
            chain(v.reciprocal(sg[:], osg[:]))
            chain(v.tensor_scalar(osg[:], sg[:], -1.0, 1.0, ALU.mult, ALU.add))
            v.wait_ge(w_in, 16 * 7)
            v.tensor_tensor(bsg[:], bp_c[:], sg[:, 4:5], ALU.mult).then_inc(sg_ready, 1)

            def norm_stats(phase, g):
                for k in range(R * g, R * g + R):
                    last = do(v.bn_stats(stats[:, k, :], X[:, k, :]))
                steps.wait(last)
                s = stats[:, R * g:R * g + R, :].rearrange("p n s -> p s n")
                l = ln[:, phase, :, R * g:R * g + R]
                a = do(v.tensor_tensor(l[:, 1, :], s[:, 1, :], s[:, 4, :], ALU.subtract))
                b = do(v.tensor_tensor(l[:, 0, :], s[:, 1, :], s[:, 4, :], ALU.add))
                c = do(v.tensor_tensor(l[:, 2, :], s[:, 2, :], s[:, 5, :], ALU.add))
                steps.wait(c)
                d = do(v.tensor_tensor(l[:, 1, :], l[:, 1, :], l[:, 1, :], ALU.mult))
                chain(v.tensor_scalar(l[:, 0, :], l[:, 0, :], 0.5, None, ALU.mult))
                v.scalar_tensor_tensor(l[:, 3, :], l[:, 1, :], C / 4.0, l[:, 2, :], ALU.mult,
                                       ALU.add).then_inc(var_ready, 1)

            def norm_spread(phase, g):
                l = ln[:, phase, :, R * g:R * g + R]
                v.wait_ge(std_ready, norm_rank[phase, g] + 1)
                v.reciprocal(l[:, 5, :], l[:, 4, :]).then_inc(rstd_ready, 1)

            def add_residual(g):
                v.wait_ge(osp_turned, g + 1)
                rows = X[:, R * g:R * g + R, :].rearrange("p n c -> p (n c)")
                v.wait_ge(xn_ready, norm_rank[0, g] + 1)
                v.tensor_tensor(rows, PS[:, PERM_BANK, :].bitcast(BF16)[:, 0:W], rows,
                                ALU.add).then_inc(res_added, 1)
                v.wait_ge(res_added, g + 1)

            v.wait_ge(w_ready, 1)
            WpT = wT[:, 3, :]
            chain(v.tensor_copy(wpT[:, 0, :], WpT))
            chain(v.tensor_tensor(wres[:, 0, :], WpT, wpT[:, 0, :], ALU.subtract))
            chain(v.tensor_copy(wpT[:, 1, :], wres[:, 0, :]))
            chain(v.tensor_tensor(wres[:, 1, :], wres[:, 0, :], wpT[:, 1, :], ALU.subtract))
            m = do(v.tensor_copy(wpT[:, 2, :], wres[:, 1, :]))
            v.sem_inc(piece_read, DEEP)
            v.sem_inc(rows_ready, AHEAD)
            steps.wait(m)
            do(v.memset(OM[:], 1.0))
            do(v.memset(U[:], 0.0))
            steps.wait(steps.count)
            for w, col in enumerate((0, 1, 2, 4)):
                do(v.tensor_scalar(OM[:, w, :], OM[:, w, :], osg[:, col:col + 1], None, ALU.mult))
            v.memset(VY[:], 0.0).then_inc(wp_split, 1)
            steps.wait(steps.count)

            def mask_kv(i):
                v.wait_ge(kv_done, i + 1)
                if i >= 2:
                    v.wait_ge(y_done, 2 * i - 2)
                src = PS[:, KV_BANK:KV_BANK + 2, :].rearrange("p h (i c) -> p h i c", i=4)
                dst = KV[i % 2][:].rearrange("p i h c -> p h i c")
                mb = mask[:].rearrange("p h d -> p (h d)").unsqueeze(1).to_broadcast([128, 8, 128])
                mb = mb.rearrange("p (h i) c -> p h i c", h=2)
                v.tensor_tensor(dst, src, mb, ALU.mult).then_inc(kv_masked, 1)

            def y_lif(t):
                v.wait_ge(perm_copied, len(PERM) * (t + 1))
                if t >= 2:
                    v.wait_ge(ring_done, item_rank["qkv", 3, BT * (t - 1) - 1, 0] + 1)
                flat = lambda a: a[:].rearrange("p n b -> p (n b)")
                chain(v.scalar_tensor_tensor(flat(HY), flat(VY), osg[:, 3:4], flat(HY), ALU.mult, ALU.add))
                v.tensor_scalar(ysp[t % 2][:].rearrange("p b n -> p n b"), HY[:], 1.0, None,
                                ALU.is_ge).then_inc(ysp_ready, 1)
                v.scalar_tensor_tensor(flat(VY), flat(HY), 1.0, flat(HY), ALU.is_lt, ALU.mult).then_inc(hy_used, 1)
                v.wait_ge(hy_used, t + 1)

            small = PS[:, GATE_BANK, 0:(R + 1) * E].rearrange("p (r e) -> p r e", e=E)
            lg = small[:, 0:R, :]
            rk = rank[:].unsqueeze(1).to_broadcast([128, R, E])
            bc = lambda a: a.unsqueeze(2).to_broadcast([128, R, E])

            def choose(g):
                d, ex, t, hit1, d2, hit2 = (gate[:, k] for k in range(6))
                top, top2, e2, r1, r2, _ = (gate1[:, k] for k in range(6))
                v.wait_ge(logits_done, g + 1)
                chain(v.tensor_reduce(top, lg, AX.X, ALU.max))
                chain(v.tensor_tensor(d, lg, bc(top), ALU.subtract))
                chain(v.scalar_tensor_tensor(t, d, 0.0, rk, ALU.is_ge, ALU.mult))
                chain(v.tensor_reduce(r1, t, AX.X, ALU.max))
                if g >= 2:
                    v.wait_ge(scattered[g % 2], 16 * 2 * R * (g // 2))
                do(v.tensor_copy(XG[g % 2][:, :, C + 1], r1))
                chain(v.tensor_tensor(hit1, t, bc(r1), ALU.is_equal))
                chain(v.scalar_tensor_tensor(d2, hit1, -1e30, d, ALU.mult, ALU.add))
                v.tensor_reduce(top2, d2, AX.X, ALU.max).then_inc(gate_in, 1)
                v.wait_ge(gate_in, g + 1)
                chain(v.tensor_tensor(t, d2, bc(top2), ALU.is_equal))
                chain(v.tensor_tensor(t, t, rk, ALU.mult))
                chain(v.tensor_reduce(r2, t, AX.X, ALU.max))
                chain(v.tensor_tensor(hit2, t, bc(r2), ALU.is_equal))
                v.tensor_tensor(chosen[:, 0:R, :], hit1, hit2, ALU.add).then_inc(chosen_ready, 1)

            def rank_rows(g):
                d, ex, t, hit1, d2, hit2, t2 = (gate[:, k] for k in range(7))
                top, top2, e2, r1, r2, den = (gate1[:, k] for k in range(6))
                share = score[:, R * g:R * g + R, :]
                v.wait_ge(gate_exp, 2 * g + 2)
                a = do(v.tensor_reduce(den, ex, AX.X, ALU.add))
                v.wait_ge(ranked, g + 1)
                b = do(v.tensor_tensor(t, small[:, 0:R, :], filled[:].unsqueeze(1).to_broadcast([128, R, E]),
                                       ALU.add))
                steps.wait(a)
                a = do(v.scalar_tensor_tensor(den, den, GATE_EPS, e2, ALU.mult, ALU.add))
                steps.wait(b)
                do(v.tensor_tensor(filled[:], small[:, R, :], filled[:], ALU.add))
                b = do(v.tensor_tensor(d2, t, hit1, ALU.mult))
                c = do(v.tensor_tensor(t2, t, hit2, ALU.mult))
                steps.wait(a)
                a = do(v.tensor_scalar(den, den, 1.0, None, ALU.add))
                if g >= 2:
                    v.wait_ge(scattered[g % 2], 16 * 2 * R * (g // 2))
                steps.wait(b)
                with nc.allow_low_precision(reason="whole numbers below 2 ** 24"):
                    v.tensor_reduce(place[g % 2][:, 0, :], d2, AX.X, ALU.add).then_inc(place_ready, 1)
                    steps.wait(c)
                    v.tensor_reduce(place[g % 2][:, 1, :], t2, AX.X, ALU.add).then_inc(place_ready, 1)
                steps.wait(a)
                chain(v.reciprocal(share[:, :, 0], den))
                chain(v.tensor_tensor(share[:, :, 1], e2, share[:, :, 0], ALU.mult))

            v.wait_ge(consts, NCONST)
            chain(v.tensor_copy(filled[:], region[:]))
            for slot in range(-1, END):
                if 0 <= slot < SLOTS:
                    lo = 0 if slot < BLOCKS else 3
                    hi = 4 if slot >= LAG else 3
                    h, cur = H[slot % 3], slice(lo, hi)
                    last = ("qkv", 3, slot - LAG, 0) if slot >= LAG else ("qkv", 2, slot, 0)
                    v.wait_ge(ring_copied, item_rank[last] + 1)
                    for st in range(SB):
                        flat = lambda a: a.rearrange("p w n -> p (w n)")
                        m = do(v.tensor_tensor(flat(h[:, st, cur, :]), flat(U[:, cur, :]), flat(h[:, st, cur, :]),
                                               ALU.add))
                        if st == 3 and 1 <= slot <= BLOCKS:
                            mask_kv(slot - 1)
                        steps.wait(m)
                        m = do(v.scalar_tensor_tensor(flat(VV[:, cur, :]), flat(h[:, st, cur, :]), 1.0,
                                                      flat(h[:, st, cur, :]), ALU.is_lt, ALU.mult))
                        steps.wait(m)
                        m = do(v.tensor_tensor(flat(U[:, cur, :]), flat(VV[:, cur, :]), flat(OM[:, cur, :]), ALU.mult))
                        if st == 5:
                            if slot % BT == 1 and 0 < slot // BT <= T:
                                y_lif(slot // BT - 1)
                        steps.wait(m)
                    if slot < BLOCKS:
                        if slot >= 2:
                            v.wait_ge(y_done, 2 * (slot - 1))
                        out_s = spikes[slot % 2][:, :, :, 0:N]
                        m = v.tensor_scalar(out_s, h[:, :, 0:3, :].rearrange("p s w n -> p w s n"), 1.0, None,
                                            ALU.is_ge)
                        m.then_inc(block_done, 1)
                    if slot >= LAG:
                        ob = slot - LAG
                        m = v.tensor_scalar(osp[:, BC * ob:BC * ob + BC].rearrange("p (s n) -> p s n", n=N),
                                            h[:, :, 3, :], 1.0, None, ALU.is_ge)
                        m.then_inc(osp_ready, 1)
                        if slot >= BLOCKS:
                            v.wait_ge(osp_ready, ob + 1)
                            v.sem_inc(block_done, 1)
                for phase, g in norms(slot):
                    if phase == 0:
                        v.wait_ge(x_ready, g + 1)
                    else:
                        add_residual(g)
                    norm_stats(phase, g)
                for x_ in norms(slot):
                    norm_spread(*x_)
                for g in gate_group(slot, 3):
                    rank_rows(g)
                for g in gate_group(slot, 2):
                    choose(g)

            spread_to = lambda a, n: a.unsqueeze(1).to_broadcast([128, n, E])
            chain(v.tensor_tensor(count1[:, 0], filled[:], region[:], ALU.subtract))
            chain(v.tensor_tensor(tally[:], counts_at[:].unsqueeze(1).to_broadcast([128, E, COUNTS]),
                                  count1[:, 0].unsqueeze(2).to_broadcast([128, E, COUNTS]), ALU.is_lt))
            chain(v.tensor_reduce(count1[:, 1], tally[:], AX.X, ALU.add))
            chain(v.tensor_tensor(tally[:, :, 0:E], upto[:], spread_to(count1[:, 1], E), ALU.mult))
            chain(v.tensor_reduce(count1[:, 2], tally[:, :, 0:E], AX.X, ALU.add))
            chain(v.tensor_scalar(count1[:, 3], count1[:, 1], -float(ROWS), float(CAP), ALU.mult, ALU.add))
            chain(v.tensor_tensor(passed[:, 0], piece_no[:].unsqueeze(2).to_broadcast([128, PIECES, E]),
                                  spread_to(count1[:, 2], PIECES), ALU.is_ge))
            chain(v.tensor_reduce(piece_f[:, 0], passed[:, 0], AX.X, ALU.add))
            chain(v.tensor_scalar(piece_f[:, 0], piece_f[:, 0], E - 1.0, None, ALU.min))
            chain(v.tensor_scalar(piece_rank[:], piece_f[:, 0], -1.0, float(E), ALU.mult, ALU.add))
            chain(v.tensor_copy(piece_expert[:], piece_f[:, 0]))
            chain(v.tensor_tensor(passed[:, 1], passed[:, 0], spread_to(count1[:, 3], PIECES), ALU.mult))
            chain(v.tensor_reduce(piece_f[:, 1], passed[:, 1], AX.X, ALU.add))
            chain(v.scalar_tensor_tensor(piece_f[:, 1], piece_no[:], float(ROWS), piece_f[:, 1], ALU.mult, ALU.add))
            chain(v.tensor_scalar(piece_start[:], piece_f[:, 1], float(E * CAP), None, ALU.min))
            chain(v.tensor_copy(region_end[:], filled[:]))
            v.wait_ge(ffn_in, 16 * 4)
            v.wait_ge(w_turned, 2)
            v.tensor_copy(b1c[:], PS[:, 1, 0:E * HB]).then_inc(pieces_ready, 1)
            v.wait_ge(pieces_ready, 1)

            def expert_of(j):
                return v.value_load(piece_expert[0:1, bass.ds(j, 1)], min_val=0, max_val=E - 1)

            def set_w1(j, b, e):
                v.wait_ge(up_done, HB * (j + 1))
                v.tensor_copy(w_now[b % 2][:, 0, :], W1_s[:].rearrange("p e h -> p (e h)")[:, bass.ds(e * HID, HID)]
                              ).then_inc(w1_set, 1)

            def copy_turned(j, b):
                v.wait_ge(piece_turned, j + 1)
                v.tensor_copy(rows_T[b % 2][:], PS[:, 6 + b % 2, 0:ROWS]).then_inc(piece_copied, 1)

            def set_w2(j, b, e):
                v.wait_ge(down_done, j + 1)
                v.tensor_copy(b1_now[b % 2][:], b1c[:, bass.ds(e * HB, HB)]).then_inc(b1_set, 1)
                v.tensor_copy(w_now[b % 2][:, 1, :],
                              W2_s[:].rearrange("p e b c -> p (e b c)")[:, bass.ds(e * HB * C, HB * C)]
                              ).then_inc(w2_set, 1)

            def set_target(j, b, n):
                v.wait_ge(piece_turned, j + 1)
                if not (isinstance(n, int) and n == 0):
                    v.wait_ge(rows_sent[b], 16 * HALVES * n)
                v.scalar_tensor_tensor(target[b][:], rows_in[b][:, :, C + 1], piece_rank[:, bass.ds(j, 1)],
                                       rows_in[b][:, :, C], ALU.not_equal, ALU.add).then_inc(piece_read, 1)

            def add_b2(j, b):
                e = expert_of(j)
                v.wait_ge(down_done, AHEAD + j + 1)
                b2_e = b2b[:].rearrange("p e c -> p (e c)")[:, bass.ds(e * C, C)]
                v.tensor_tensor(rows_out[b], PS[:, 4 + b % 2, 0:ROWS].rearrange("p (a c) -> p a c", a=HALVES),
                                b2_e.unsqueeze(1).to_broadcast([128, HALVES, C]), ALU.add).then_inc(rows_ready, 1)

            def set_up(j, b, n):
                e = expert_of(j)
                set_w1(j, b, e)
                copy_turned(j, b)
                set_w2(j, b, e)
                set_target(j, b, n)

            def next_piece(j, b, n):
                b2, n2 = (b + AHEAD) % DEEP, n + (b + AHEAD) // DEEP
                e = expert_of(j + AHEAD)
                set_w1(j + AHEAD, b2, e)
                copy_turned(j + AHEAD, b2)
                add_b2(j, b)
                set_w2(j + AHEAD, b2, e)
                set_target(j + AHEAD, b2, n2)

            for j in range(AHEAD):
                set_up(j, j, 0)
            for b in range(DEEP):
                next_piece(b, b, 0)
            with v.Fori(1, PIECES // DEEP - 1) as i:
                for b in range(DEEP):
                    next_piece(DEEP * i + b, b, i)
            for b in range(DEEP - AHEAD):
                next_piece(PIECES - DEEP + b, b, PIECES // DEEP - 1)
            for b in range(DEEP - AHEAD, DEEP):
                add_b2(PIECES - DEEP + b, b)

            for g in range(G):
                v.wait_ge(shares_in[g], 16)
                for k in range(2):
                    for r in range(R):
                        n = R * g + r
                        m = v.scalar_tensor_tensor(X[:, n, :], shares[g][:, r, k, :], score[:, n, k:k + 1], X[:, n, :],
                                                   ALU.mult, ALU.add)
                        if k == 0:
                            do(m)
                    if k == 0:
                        steps.wait(steps.count)
                m.then_inc(out_ready, 1)

        @block.tensor
        def _(pe):
            pe.wait_ge(consts, NCONST)
            pe.wait_ge(w_in, 16 * 7)
            for i in range(4):
                m = pe.transpose(PS[:, 0, i * 128:i * 128 + 128], wrow[:, i, :], identf[:])
            m.then_inc(w_turned, 1)
            pe.wait_ge(w_ready, 1)

            def ring_item(item):
                kind, w, b, c = item
                n = item_rank[item]
                bank = PS[:, RING + n % 2, :]
                if n >= 2:
                    pe.wait_ge(ring_copied, n - 1)
                if kind == "turn":
                    k0, k1 = CUTS[c]
                    src = XG[b % 2] if w else XN
                    pe.wait_ge(xn_ready, norm_rank[w, b] + 1)
                    for r in range(k0, k1):
                        m = pe.transpose(bank[:, (r - k0) * 128:(r - k0) * 128 + 128], src[:, r, 0:C], identf[:])
                    m.then_inc(ring_done, 1)
                    if c:
                        pe.wait_ge(ring_done, n + 1)
                        pe.sem_inc(xt_turned, 1)
                elif w < 3:
                    g = (BC * (b + 1) - 1) // W
                    pe.wait_ge(ring_copied, item_rank["turn", 0, g, 1] + 1)
                    pe.matmul(bank[:, 0:BC], wT[:, w, :], xT[:, BC * b:BC * b + BC], start=True,
                              stop=True).then_inc(ring_done, 1)
                else:
                    t = b // BT
                    pe.wait_ge(ysp_ready, t + 1)
                    src = ysp[t % 2][:, SB * (b % BT):SB * (b % BT) + SB, :].rearrange("p b n -> p (b n)")
                    for part in range(3):
                        m = pe.matmul(bank[:, 0:BC], wpT[:, part, :], src, start=(part == 0), stop=(part == 2))
                    m.then_inc(ring_done, 1)

            def pair(w, p):
                p *= 2
                return spikes[p // SB % 2][:, w, p % SB:p % SB + 2, :].rearrange("p h n -> p (h n)")

            def turn_kv(i):
                pe.wait_ge(block_done, i + 1)
                if i:
                    pe.wait_ge(kvt_copied, i)
                bank = PS[:, KVT_BANK, :].bitcast(BF16)
                for w in range(2):
                    for a in range(4):
                        k = (w * 4 + a) * 128
                        m = pe.transpose(bank[:, k:k + 128], pair(1 + w, 4 * i + a), identb[:])
                m.then_inc(kvt_turned, 1)

            def key_value(i):
                pe.wait_ge(kvt_copied, i + 1)
                if i:
                    pe.wait_ge(kv_masked, i)
                for a in range(4):
                    for par in range(2):
                        rows = slice(64 * par, 64 * par + N)
                        m = pe.matmul(PS[:, KV_BANK + par, a * 128:a * 128 + 128], KVT[i % 2][rows, 0, a, :],
                                      KVT[i % 2][rows, 1, a, :], start=True, stop=True)
                m.then_inc(kv_done, 1)

            def query(i):
                pe.wait_ge(kv_masked, i + 1)
                for half in range(2):
                    if 2 * i + half:
                        pe.wait_ge(y_copied, 2 * (2 * i + half))
                    for a in range(2):
                        m = pe.matmul(PS[:, Y_BANK, a * 256:a * 256 + 256], pair(0, 4 * i + 2 * half + a),
                                      KV[i % 2][:, 2 * half + a, :, :].rearrange("p h c -> p (h c)"), start=True,
                                      stop=True)
                    m.then_inc(y_done, 1)

            perm_bank_users = [0, 0]

            def permute(t):
                pe.wait_ge(y_copied, 4 * BT * (t + 1))
                if perm_bank_users[1]:
                    pe.wait_ge(res_added, perm_bank_users[1])
                for n0, n1 in PERM:
                    if perm_bank_users[0]:
                        pe.wait_ge(perm_copied, perm_bank_users[0])
                    perm_bank_users[0] += 1
                    for n in range(n0, n1):
                        chans = range(128 * n // N, (128 * n + 127) // N + 1)
                        for par in range(2):
                            col = ((n - n0) * 2 + par) * (B // 2)
                            for ch in chans:
                                s = N * ch - 128 * n
                                m = pe.matmul(PS[:, PERM_BANK, col:col + B // 2],
                                              shift[:, par, 127 - s:255 - s],
                                              Y[:, ch, t * B // 2:(t + 1) * B // 2], start=(ch == chans[0]),
                                              stop=(ch == chans[-1]))
                    m.then_inc(perm_done, 1)

            def turn_out(g):
                pe.wait_ge(osp_ready, norm2_block(g) + 1)
                if perm_bank_users[0]:
                    pe.wait_ge(perm_copied, perm_bank_users[0])
                if perm_bank_users[1]:
                    pe.wait_ge(res_added, perm_bank_users[1])
                perm_bank_users[1] += 1
                for r in range(R):
                    k = R * g + r
                    m = pe.transpose(PS[:, PERM_BANK, :].bitcast(BF16)[:, r * 128:r * 128 + 128],
                                     osp[:, k * 128:k * 128 + 128], identb[:])
                m.then_inc(osp_turned, 1)

            small = PS[:, GATE_BANK, 0:(R + 1) * E].rearrange("p (r e) -> p r e", e=E)

            def logits(g):
                pe.wait_ge(ring_copied, item_rank["turn", 1, g, 1] + 1)
                if g:
                    pe.wait_ge(place_ready, 2 * g)
                for r in range(R):
                    n = R * g + r
                    m = pe.matmul(small[:, r, :], xT[:, n * 128:n * 128 + 128], Wg_s[:], start=True, stop=True)
                m.then_inc(logits_done, 1)

            def count_before(g):
                pe.wait_ge(chosen_ready, g + 1)
                pe.matmul(small, before[:], chosen[:], start=True, stop=False)
                for r in range(R):
                    m = pe.matmul(small[:, r + 1:R + 1, :], all_ones[:],
                                  chosen[:, r:r + 1, :].to_broadcast([128, R - r, E]), start=False, stop=(r == R - 1))
                m.then_inc(ranked, 1)

            pe.sem_inc(up_done, AHEAD * HB)
            pe.sem_inc(down_done, AHEAD)
            pe.wait_ge(wp_split, 1)
            for slot in range(-1, END):
                for phase, g in norms(slot):
                    if phase:
                        turn_out(g)
                for it in ring[slot]:
                    ring_item(it)
                if 1 <= slot <= BLOCKS:
                    turn_kv(slot - 1)
                    key_value(slot - 1)
                    query(slot - 1)
                    if slot % BT == 0:
                        permute(slot // BT - 1)
                for g in gate_group(slot, 3):
                    count_before(g)
                for g in gate_group(slot, 1):
                    logits(g)

            pe.wait_ge(ffn_in, 16 * 4)
            pe.wait_ge(ring_copied, len(item_rank))
            pe.transpose(PS[:, 1, 0:E * HB], b1r[:], identf[0:E * HB, 0:E * HB]).then_inc(w_turned, 1)

            def turn_piece(j, b, n):
                pe.wait_ge(piece_in[b], 16 * (n + 1))
                for a in range(HALVES):
                    m = pe.transpose(PS[:, 6 + b % 2, a * 128:a * 128 + 128], rows_in[b][:, a, 0:C], identf[:])
                m.then_inc(piece_turned, 1)

            def up(j, b, after_first=True):
                pe.wait_ge(w1_set, j + 1)
                pe.wait_ge(piece_copied, j + 1)
                for hb in range(HB):
                    if after_first:
                        pe.wait_ge(gelu_done, HB * (j - 1) + hb + 1)
                    pe.matmul(PS[:, hb, 0:ROWS], w_now[b % 2][:, 0, hb * 128:hb * 128 + 128],
                              rows_T[b % 2][:], start=True, stop=True).then_inc(up_done, 1)

            def down(j, b):
                pe.wait_ge(w2_set, j + 1)
                pe.wait_ge(rows_ready, j + 1)
                pe.wait_ge(gelu_done, HB * (j + 1))
                for a in range(HALVES):
                    for hb in range(HB):
                        m = pe.matmul(PS[:, 4 + b % 2, a * 128:a * 128 + 128], hid[b % 2][:, hb, a * 128:a * 128 + 128],
                                      w_now[b % 2][:, 1, hb * C:hb * C + C], start=(hb == 0), stop=(hb == HB - 1))
                m.then_inc(down_done, 1)

            turn_piece(0, 0, 0)
            turn_piece(1, 1, 0)
            up(0, 0, after_first=False)

            def next_products(j, b, n):
                turn_piece(j + AHEAD, (b + AHEAD) % DEEP, n + (b + AHEAD) // DEEP)
                up(j + 1, (b + 1) % DEEP)
                down(j, b)

            with pe.Fori(0, PIECES // DEEP - 1) as i:
                for b in range(DEEP):
                    next_products(DEEP * i + b, b, i)
            for b in range(DEEP - AHEAD):
                next_products(PIECES - DEEP + b, b, PIECES // DEEP - 1)
            up(PIECES - 1, DEEP - 1)
            down(PIECES - 2, DEEP - 2)
            down(PIECES - 1, DEEP - 1)


_INS = ["x", "L0_conv_Wq", "L0_conv_Wk", "L0_conv_Wv", "L0_conv_Wp", "L0_conv_bp", "lif_w", "L0_ffn_Wg",
        "L0_ffn_W1", "L0_ffn_b1", "L0_ffn_W2", "L0_ffn_b2"]


def kernel(**inputs):
    import numpy as np
    import concourse.bacc as bacc
    from concourse import mybir as mb
    from concourse.bass_utils import run_bass_kernel_spmd

    lifs = [np.reshape(inputs[f"L0_conv_{n}"], (1,)) for n in ("wq", "wk", "wv", "wa", "wp")]
    inputs = {**inputs, "lif_w": np.concatenate(lifs)}
    nc = bacc.Bacc("TRN2", target_bir_lowering=False, num_devices=1)
    arrays, args = {}, []
    for name in _INS:
        a = np.ascontiguousarray(inputs[name])
        arrays[f"in_{name}"] = a
        args.append(nc.dram_tensor(f"in_{name}", a.shape, mb.dt.from_np(a.dtype), kind="ExternalInput").ap())
    out = nc.dram_tensor("out", inputs["x"].shape, mb.dt.float32, kind="ExternalOutput").ap()
    metaformer_block(nc, *args, out)
    r = run_bass_kernel_spmd(nc, [arrays], core_ids=[0])
    return r.results[0]["out"]
```

```python
from contextlib import ExitStack

import concourse.bass as bass
from concourse import mybir

ALU = mybir.AluOpType
ACT = mybir.ActivationFunctionType
AX = mybir.AxisListType
F32 = mybir.dt.float32
BF16 = mybir.dt.bfloat16
F32R = mybir.dt.float32r
I32 = mybir.dt.int32
F16 = mybir.dt.float16


class Steps:

    def __init__(self, engine, semaphore):
        self.engine, self.semaphore, self.base, self.count = engine, semaphore, 0, 0

    def mark(self, instruction):
        instruction.then_inc(self.semaphore, 1)
        self.count += 1
        return self.count

    def wait(self, mark):
        self.engine.wait_ge(self.semaphore, self.base + mark)


def metaformer_block(nc, x, Wq, Wk, Wv, Wp, bp, lif_w, Wg, W1, b1, W2, b2, out):
    T, B, N, C = x.shape
    TB = T * B
    E, _, HID = W1.shape
    HB = HID // 128
    HEADS = 8
    D = C // HEADS
    NPAD = 64
    PAIRS = TB // 2
    LN1_EPS, LN2_EPS, GATE_EPS = 1e-6, 1e-5, 1e-6
    TOK = TB * N
    TILES = TOK // 128
    R = 7
    G = TILES // R
    SB = 8
    BLOCKS = TB // SB
    BC = SB * N
    LAG = 7
    SLOTS = BLOCKS + LAG
    assert C == 128 and TB == 128 and HID % 128 == 0 and TOK % (128 * R) == 0 and N <= NPAD and BC <= 512
    W = R * 128
    CUTS = [(0, 4), (4, R)]
    BT = BLOCKS // T
    CHOOSE_FROM = 11
    Y_PARTS = 7
    Y_PART = N // Y_PARTS
    assert N % Y_PARTS == 0 and Y_PARTS <= SB
    ROWS = 256
    SENDING = 3
    HALVES = ROWS // 128
    CAP = TOK + ROWS
    PIECES = 2 * TOK // ROWS + E - 1
    PIECES += -PIECES % 4
    PAYLOAD = C + 2
    SKIPPED = 2.0 ** 20
    COUNTS = -(-TOK // ROWS)
    assert 2 * TOK % ROWS == 0
    AHEAD = 2
    DEEP = 4
    assert PIECES % DEEP == 0

    x_v = x.rearrange("t b n c -> (t b n) c").rearrange("(k p) c -> p k c", p=128)
    out_v = out.rearrange("t b n c -> (t b n) c").rearrange("(k p) c -> p k c", p=128)

    def norm1_block(g):
        return W * g // BC

    def norm2_block(g):
        return (W * (g + 1) - 1) // BC

    norm1_slot = {g: norm1_block(g) - 3 for g in range(G)}
    norm2_slot = {g: norm2_block(g) + LAG + 1 for g in range(G)}
    END = max(norm2_slot.values()) + 4

    def gate_group(slot, behind):
        return [g for g in range(G) if norm2_slot[g] + behind == slot]

    def ring_items(slot):
        early, late = [], []
        for g in range(G):
            if max(norm1_slot[g] + 1, -1) == slot:
                (early if slot < 0 else late).extend([("turn", 0, g, c) for c in range(2)])
        if slot + 1 < BLOCKS:
            early += [("qkv", w, slot + 1, 0) for w in range(3)]
        if 0 <= slot + 1 - LAG < BLOCKS:
            late.insert(0, ("qkv", 3, slot + 1 - LAG, 0))
        for g in gate_group(slot, 1):
            late += [("turn", 1, g, c) for c in range(2)]
        return early, late

    def moves(slot, late):
        t, c = slot // BT - 1, slot % BT
        if not 0 <= t < T:
            return []
        if t == T - 1:
            return {(0, True): [(t, 0), (t, 1)], (1, False): [(t, 2), (t, 3)]}.get((c, late), [])
        return {(0, True): [(t, 0)], (1, True): [(t, 1), (t, 2)], (2, False): [(t, 3)]}.get((c, late), [])

    def norms(slot):
        return ([(0, g) for g in range(G) if max(norm1_slot[g], -1) == slot]
                + [(1, g) for g in range(G) if norm2_slot[g] == slot])

    ON_VECTOR = [(0, 0)]
    ON_SCALAR = [(1, g) for g in range(G) if norm2_slot[g] > BLOCKS]

    norm_order = [x for s in range(-1, END) for x in norms(s)]
    norm_rank = {x: i for i, x in enumerate(norm_order)}
    item_rank, ring = {}, {}
    for s in range(-1, END):
        ring[s] = ring_items(s)
        for it in ring[s][0] + ring[s][1]:
            item_rank[it] = len(item_rank)

    ctx = ExitStack()
    with ctx:
        def sb(name, shape, dt=F32):
            return ctx.enter_context(nc.sbuf_tensor(name, shape, dt))

        def sem(name):
            return ctx.enter_context(nc.semaphore(name))

        PS = ctx.enter_context(nc.psum_tensor("PS", [128, 8, 512], F32))
        RING, KVT_BANK, KV_BANK, Y_BANK, GATE_BANK, PERM_BANK = 0, 2, 3, 5, 6, 7

        X = sb("X", [128, TILES, C])
        XD = sb("XD", [128, R, C])
        XN = sb("XN", [128, R, C])
        xT = sb("xT", [128, TOK])
        spikes = [sb(f"spikes{i}", [128, 3, SB, NPAD], BF16) for i in range(2)]
        H_all = sb("H_all", [128, 3, 4, SB, N])
        H = [H_all[:, i] for i in range(3)]
        U = sb("U", [128, 4, N])
        VV = sb("VV", [128, 4, N])
        OM = sb("OM", [128, 4, N])
        KVT = [sb(f"KVT{i}", [128, 2, 4, 128], BF16) for i in range(2)]
        KV = [sb(f"KV{i}", [128, 4, 2, 128], BF16) for i in range(2)]
        Y = sb("Y", [128, C, PAIRS], F16)
        HY = sb("HY", [128, N, B])
        VY = sb("VY", [128, N, B])
        ysp = [sb(f"ysp{i}", [128, N, B], BF16) for i in range(2)]
        osp = sb("osp", [128, TOK], BF16)
        shift = sb("shift", [128, 2, 304], F16)
        mask = sb("mask", [128, HEADS, D])
        identf = sb("identf", [128, 128])
        identb = sb("identb", [128, 128], BF16)
        ones = HY[:].rearrange("p n b -> p (n b)")[:, 0:608].rearrange("p (a b) -> p a b", a=2)
        wrow = HY[:].rearrange("p n b -> p (n b)")[:, 608:1120].rearrange("p (a b) -> p a b", a=4)
        wT = sb("wT", [128, 4, C])
        wpT = sb("wpT", [128, 3, C], BF16)
        weight_rest = VY[:].rearrange("p n b -> p (n b)")[:, 0:2 * C].rearrange("p (a b) -> p a b", a=2)
        bp_c = sb("bp_c", [128, 1])
        bsg = sb("bsg", [128, 1])
        lw = sb("lw", [128, 5])
        sg = sb("sg", [128, 5])
        osg = sb("osg", [128, 5])
        stats = sb("stats", [128, TILES, 6])
        ln = sb("ln", [128, 2, 6, TILES])
        Wg_s = sb("Wg_s", [128, E])
        W2_s = sb("W2_s", [128, E, HB, C])
        b1r = sb("b1r", [E * HB, 128])
        b1c = sb("b1c", [128, E * HB])
        b2b = sb("b2b", [128, E, C])
        rank = sb("rank", [128, E])
        score = sb("score", [128, TILES, 2])
        XG = [sb(f"XG{i}", [128, R, PAYLOAD]) for i in range(SENDING)]
        w1_high = [sb(f"w1_high{i}", [128, HID], F32R) for i in range(2)]
        w1_low = [sb(f"w1_low{i}", [128, HID], F32R) for i in range(2)]
        rows_high = [sb(f"rows_high{i}", [128, ROWS], F32R) for i in range(2)]
        rows_low = [sb(f"rows_low{i}", [128, ROWS], F32R) for i in range(2)]
        pad_rows = sb("pad_rows", [128, HALVES, PAYLOAD])
        twice_token = sb("twice_token", [128, TILES])
        gate = sb("gate", [128, 7, R, E])
        gate1 = sb("gate1", [128, 6, R])
        chosen = sb("chosen", [128, R + 1, E], BF16)
        before = sb("before", [128, 128], BF16)
        all_ones = sb("all_ones", [128, 128], BF16)
        filled = sb("filled", [128, E])
        place = [sb(f"place{i}", [128, 2, R], I32) for i in range(SENDING)]
        upto = sb("upto", [128, E, E])
        region = sb("region", [128, E])
        counts_at = sb("counts_at", [128, COUNTS])
        piece_no = sb("piece_no", [128, PIECES])
        count1 = sb("count1", [128, 5, E])
        piece_rank = sb("piece_rank", [128, PIECES])
        piece_f = sb("piece_f", [128, 2, PIECES])
        piece_expert = sb("piece_expert", [128, PIECES], I32)
        piece_start = sb("piece_start", [128, PIECES], I32)
        region_end = sb("region_end", [128, E], I32)
        rows_in = [sb(f"rows_in{i}", [128, HALVES, PAYLOAD]) for i in range(DEEP)]
        target = [sb(f"target{i}", [128, HALVES], I32) for i in range(DEEP)]
        lneps1 = sb("lneps1", [128, 1])
        lneps2 = sb("lneps2", [128, 1])
        potentials_memory = Y[:].rearrange("p c n -> p (c n)").bitcast(F32)
        hid = [potentials_memory[:, i * HB * ROWS:(i + 1) * HB * ROWS].rearrange("p (b c) -> p b c", b=HB) for i in range(2)]
        w2_now = [potentials_memory[:, 2 * HB * ROWS + i * HB * C:2 * HB * ROWS + (i + 1) * HB * C] for i in range(2)]
        rows_out = [osp[:].bitcast(F32)[:, i * ROWS:(i + 1) * ROWS].rearrange("p (a c) -> p a c", a=HALVES)
                    for i in range(DEEP)]
        spare = VY[:].rearrange("p n b -> p (n b)")
        passed = spare[:, 0:2 * PIECES * E].rearrange("p (k j e) -> p k j e", k=2, e=E)
        tally = spare[:, 2 * PIECES * E:2 * PIECES * E + E * COUNTS].rearrange("p (e m) -> p e m", e=E)
        W1_s = H_all[:].rearrange("p i w s n -> p (i w s n)")[:, 0:E * HID].rearrange("p (e h) -> p e h", e=E)
        shares = ([xT[:, i * 2 * W:(i + 1) * 2 * W] for i in range(3)]
                  + [W1_s.rearrange("p e h -> p (e h)")[:, i * 2 * W:(i + 1) * 2 * W] for i in range(2)]
                  + [W2_s[:].rearrange("p e b c -> p (e b c)")[:, i * 2 * W:(i + 1) * 2 * W] for i in range(2)])
        shares = [a.rearrange("p (n k c) -> p n k c", k=2, c=C) for a in shares]
        by_expert = nc.dram_tensor("by_expert", (E * CAP + ROWS, PAYLOAD), F32, kind="Internal").ap()
        by_token = nc.dram_tensor("by_token", (2 * TOK, C), F32, kind="Internal").ap()
        by_token_v = by_token.rearrange("(n p k) c -> p n k c", p=128, k=2)

        x_in = [sem(f"x_in{g}") for g in range(G)]
        y_zeroed = sem("y_zeroed")
        w_in = sem("w_in")
        ffn_in = sem("ffn_in")
        w1_in = sem("w1_in")
        consts = sem("consts")
        dve = sem("dve_step")
        pools = sem("pool_step")
        lw_exp = sem("lw_exp")
        sg_ready = sem("sg_ready")
        w_turned = sem("w_turned")
        w_ready = sem("w_ready")
        wp_split = sem("wp_split")
        var_ready = sem("var_ready")
        std_ready = sem("std_ready")
        rstd_ready = sem("rstd_ready")
        shift_ready = sem("shift_ready")
        xn_ready = sem("xn_ready")
        xt_turned = sem("xt_turned")
        ring_done = sem("ring_done")
        ring_copied = sem("ring_copied")
        block_done = sem("block_done")
        kvt_turned = sem("kvt_turned")
        kvt_copied = sem("kvt_copied")
        kv_done = sem("kv_done")
        kv_masked = sem("kv_masked")
        y_done = sem("y_done")
        y_copied = sem("y_copied")
        perm_done = sem("perm_done")
        perm_copied = sem("perm_copied")
        hy_used = sem("hy_used")
        ysp_ready = sem("ysp_ready")
        osp_ready = sem("osp_ready")
        osp_turned = sem("osp_turned")
        res_added = sem("res_added")
        logits_done = sem("logits_done")
        gate_in = sem("gate_in")
        gate_exp = sem("gate_exp")
        logits_used = sem("logits_used")
        chosen_ready = sem("chosen_ready")
        first_ready = sem("first_ready")
        filled_ready = sem("filled_ready")
        ranked = sem("ranked")
        place_ready = sem("place_ready")
        scattered = [sem(f"scattered{i}") for i in range(SENDING)]
        pieces_ready = sem("pieces_ready")
        padded = sem("padded")
        piece_in = [sem(f"piece_in{i}") for i in range(DEEP)]
        piece_read = sem("piece_read")
        piece_turned = sem("piece_turned")
        piece_copied = sem("piece_copied")
        w1_set = sem("w1_set")
        w2_set = sem("w2_set")
        up_done = sem("up_done")
        gelu_done = sem("gelu_done")
        down_done = sem("down_done")
        rows_ready = sem("rows_ready")
        rows_taken = sem("rows_taken")
        rows_sent = [sem(f"rows_sent{i}") for i in range(DEEP)]
        shares_in = [sem(f"shares_in{g}") for g in range(G)]
        second_weighed = sem("second_weighed")
        out_ready = sem("out_ready")
        stored = sem("stored")

        block = ctx.enter_context(nc.Block())
        def move_bank(t, c):
            return PERM_BANK if t < T - 1 or c == 0 else KVT_BANK + c - 1

        PERM = [(n, min(n + 14, N)) for n in range(0, N, 14)]

        @block.sync
        def _(sp):
            load_x = lambda g: sp.dma_start(X[:, R * g:R * g + R, :], x_v[:, R * g:R * g + R, :])
            load_x(0).then_inc(x_in[0], 16)
            sp.wait_ge(w_in, 16 * 7)
            for g in range(1, G):
                load_x(g).then_inc(x_in[g], 16)
            sp.dma_start(W2_s[:], W2.rearrange("e (b h) c -> h e b c", h=128)).then_inc(ffn_in, 16)
            sp.dma_start(b1r[:], b1.rearrange("e (b h) -> (e b) h", h=128)).then_inc(ffn_in, 16)
            sp.dma_start(b2b[:], b2.rearrange("e c -> (e c)").partition_broadcast(128)
                         .rearrange("p (e c) -> p e c", c=C)).then_inc(ffn_in, 16)
            sp.wait_ge(osp_ready, BLOCKS)
            sp.dma_start(W1_s, W1.rearrange("e c h -> c e h")).then_inc(w1_in, 16)
            sp.wait_ge(pieces_ready, 1)
            pad_src = pad_rows[:]
            for e in range(E):
                end = sp.value_load(region_end[0:1, e:e + 1], min_val=e * CAP, max_val=e * CAP + TOK)
                sp.dma_start(by_expert[bass.ds(end, ROWS), :].rearrange("(p a) c -> p a c", a=HALVES),
                             pad_src).then_inc(padded, 16)
            sp.dma_start(by_expert[E * CAP:E * CAP + ROWS, :].rearrange("(p a) c -> p a c", a=HALVES),
                         pad_src).then_inc(padded, 16)
            sp.wait_ge(padded, 16 * (E + 1))
            for i in range(SENDING):
                sp.wait_ge(scattered[i], 16 * 2 * R * ((G - i + SENDING - 1) // SENDING))
            with sp.Fori(0, PIECES // DEEP) as i:
                for b in range(DEEP):
                    start = sp.value_load(piece_start[0:1, bass.ds(DEEP * i + b, 1)], min_val=0, max_val=E * CAP)
                    sp.wait_ge(piece_read, DEEP * i + b + 1)
                    sp.dma_start(rows_in[b][:], by_expert[bass.ds(start, ROWS), :]
                                 .rearrange("(p a) c -> p a c", a=HALVES)).then_inc(piece_in[b], 16)
            for b in range(DEEP):
                sp.wait_ge(rows_sent[b], 16 * HALVES * (PIECES // DEEP))
            sp.wait_ge(down_done, PIECES + AHEAD)
            for g in range(G):
                sp.dma_start(shares[g], by_token_v[:, R * g:R * g + R]).then_inc(shares_in[g], 16)
            for g in range(G):
                sp.wait_ge(out_ready, g + 1)
                sp.dma_start(out_v[:, R * g:R * g + R, :], X[:, R * g:R * g + R, :]).then_inc(stored, 16)
            sp.wait_ge(stored, 16 * G)

        @block.gpsimd
        def _(pool):
            steps = Steps(pool, pools)
            steps.mark(pool.memset(ones, 1.0))
            steps.mark(pool.memset(spikes[0][:, :, :, N:NPAD], 0.0))
            steps.mark(pool.memset(spikes[1][:, :, :, N:NPAD], 0.0))
            steps.wait(3)
            one = ones[:, 0, 0:128]
            pool.affine_select(out=identf[:], in_=one, compare_op=ALU.is_equal, fill=0.0, base=0,
                               pattern=[[-1, 128]], channel_multiplier=1).then_inc(consts, 1)
            pool.affine_select(out=identb[:], in_=one, compare_op=ALU.is_equal, fill=0.0, base=0,
                               pattern=[[-1, 128]], channel_multiplier=1).then_inc(consts, 1)
            pool.affine_select(out=shift[:], in_=ones, compare_op=ALU.is_equal, fill=0.0, base=127,
                               pattern=[[-64, 2], [-1, 304]], channel_multiplier=1).then_inc(pools, 1)
            steps.count += 1
            steps.wait(steps.count)
            pool.memset(shift[64:128, 0, :], 0.0).then_inc(consts, 1)
            pool.memset(shift[0:64, 1, :], 0.0).then_inc(consts, 1)
            pool.wait_ge(consts, 4)
            m1 = pool.affine_select(out=mask[:], in_=ones[:, 0, 0:128].rearrange("p (h d) -> p h d", d=D),
                                    compare_op=ALU.is_ge, fill=0.0, base=0,
                                    pattern=[[-D, HEADS], [0, D]], channel_multiplier=1)
            m = steps.mark(m1)
            steps.wait(m)
            pool.affine_select(out=mask[:], in_=mask[:], compare_op=ALU.is_ge, fill=0.0, base=D - 1,
                               pattern=[[D, HEADS], [0, D]], channel_multiplier=-1).then_inc(consts, 1)
            pool.iota(rank[:], pattern=[[-1, E]], base=E, channel_multiplier=0,
                      allow_small_or_imprecise_dtypes=True).then_inc(consts, 1)
            pool.memset(all_ones[:], 1.0).then_inc(consts, 1)
            pool.affine_select(out=before[:], in_=one, compare_op=ALU.is_ge, fill=0.0, base=-1,
                               pattern=[[1, 128]], channel_multiplier=-1).then_inc(consts, 1)
            pool.affine_select(out=upto[:], in_=ones[:, 0, 0:E * E].rearrange("p (e f) -> p e f", f=E),
                               compare_op=ALU.is_ge, fill=0.0, base=0, pattern=[[1, E], [-1, E]],
                               channel_multiplier=0).then_inc(consts, 1)
            for table, pattern, channel in ((twice_token, [[256, TILES]], 2), (region, [[CAP, E]], 0),
                                            (counts_at, [[ROWS, COUNTS]], 0), (piece_no, [[1, PIECES]], 0)):
                pool.iota(table[:], pattern=pattern, base=0, channel_multiplier=channel,
                          allow_small_or_imprecise_dtypes=True).then_inc(consts, 1)
            pool.memset(chosen[:], 0.0).then_inc(consts, 1)
            m = steps.mark(pool.memset(pad_rows[:], 0.0))
            steps.wait(m)
            pool.memset(pad_rows[:, :, C:C + 1], SKIPPED).then_inc(consts, 1)
            pool.memset(Y[:], 0.0).then_inc(y_zeroed, 1)

            def normalise(phase, g):
                k = norm_rank[phase, g]
                rows = X[:, R * g:R * g + R, :]
                bc = lambda row: ln[:, phase, row, R * g:R * g + R].unsqueeze(2).to_broadcast([128, R, C])
                pool.wait_ge(rstd_ready, k + 1)
                if k:
                    pool.wait_ge(xn_ready, k)
                m = steps.mark(pool.tensor_tensor(XD[:], rows, bc(0), ALU.subtract))
                steps.wait(m)
                if phase == 0:
                    if g:
                        pool.wait_ge(xt_turned, max(norm_rank[0, g - 1] + 1, 1))
                    dst = XN[:]
                else:
                    if g >= SENDING:
                        pool.wait_ge(scattered[g % SENDING], 16 * 2 * R * (g // SENDING))
                        pool.wait_ge(xt_turned, norm_rank[1, g - SENDING] + 1)
                    m = steps.mark(pool.tensor_copy(XG[g % SENDING][:, :, C], twice_token[:, R * g:R * g + R]))
                    steps.wait(m)
                    dst = XG[g % SENDING][:, :, 0:C]
                pool.tensor_tensor(dst, XD[:], bc(5), ALU.mult).then_inc(xn_ready, 1)

            def scatter(g):
                pool.wait_ge(place_ready, 2 * g + 2)
                pool.wait_ge(first_ready, g + 1)
                pool.wait_ge(xn_ready, norm_rank[1, g] + 1)
                for r in range(R):
                    for k in range(2):
                        pool.indirect_dma_start(by_expert, bass.IndirectOffsetOnAxis(
                            ap=place[g % SENDING][:, k, r:r + 1], axis=0), XG[g % SENDING][:, r, :], None).then_inc(scattered[g % SENDING], 16)

            for slot in range(-1, END):
                for g in gate_group(slot, 3):
                    scatter(g)
                for x_ in norms(slot):
                    if x_ not in ON_VECTOR + ON_SCALAR:
                        normalise(*x_)

            last_row = pool.alloc_register("last_row")
            pool.reg_mov(last_row, 2 * TOK - 1)
            with pool.Fori(0, PIECES // DEEP) as i:
                for b in range(DEEP):
                    pool.wait_ge(piece_read, DEEP * (i + 1) + b + 1)
                    pool.wait_ge(rows_ready, AHEAD + DEEP * i + b + 1)
                    pool.sem_inc(rows_taken, 1)
                    for a in range(HALVES):
                        pool.indirect_dma_start(by_token, bass.IndirectOffsetOnAxis(
                            ap=target[b][:, a:a + 1], axis=0), rows_out[b][:, a, :], None,
                            bounds_check=last_row, oob_is_err=False).then_inc(rows_sent[b], 16)

        NCONST = 15

        @block.scalar
        def _(act):
            with nc.allow_non_contiguous_dma(reason="a column of biases"):
                for i, w in enumerate((Wq, Wk, Wv, Wp)):
                    act.dma_start(wrow[:, i, :], w).then_inc(w_in, 16)
                act.dma_start(lw[:], lif_w.partition_broadcast(128)).then_inc(w_in, 16)
                act.dma_start(bp_c[:], bp.rearrange("(c a) -> c a", a=1)).then_inc(w_in, 16)
                act.dma_start(Wg_s[:], Wg).then_inc(w_in, 16)
            act.wait_ge(w_in, 16 * 7)
            nc.scalar.activation(sg[:], lw[:], ACT.Exp, scale=-1.0).then_inc(lw_exp, 1)

            def spread(phase, g):
                act.wait_ge(var_ready, norm_rank[phase, g] + 1)
                cols = slice(R * g, R * g + R)
                nc.scalar.activation(ln[:, phase, 4, cols], ln[:, phase, 3, cols], ACT.Sqrt,
                                     bias=(lneps1, lneps2)[phase][:], scale=1.0 / C).then_inc(std_ready, 1)

            def scale_rows(g):
                act.wait_ge(shift_ready, ON_SCALAR.index((1, g)) + 1)
                act.wait_ge(scattered[g % SENDING], 16 * 2 * R * (g // SENDING))
                act.wait_ge(xt_turned, norm_rank[1, g - SENDING] + 1)
                for k in range(R):
                    n = R * g + k
                    m = nc.scalar.activation(XG[g % SENDING][:, k, 0:C], X[:, n, :], ACT.Identity,
                                             scale=ln[:, 1, 5, n:n + 1], bias=ln[:, 1, 1, n:n + 1])
                m.then_inc(xn_ready, 1)

            def copy_item(item):
                kind, w, b, c = item
                n = item_rank[item]
                act.wait_ge(ring_done, n + 1)
                bank = PS[:, RING + n % 2, :]
                if kind == "turn":
                    k0, k1 = (R * b + x for x in CUTS[c])
                    nc.scalar.activation(xT[:, 128 * k0:128 * k1], bank[:, 0:128 * (k1 - k0)],
                                         ACT.Copy).then_inc(ring_copied, 1)
                    return
                slot = b + (LAG if w == 3 else 0)
                if slot >= 3:
                    act.wait_ge(block_done, slot - 2)
                dst = H[slot % 3][:, w].rearrange("p s n -> p (s n)")
                src = bank[:, 0:BC]
                if w == 3:
                    nc.scalar.activation(dst, src, ACT.Identity, scale=sg[:, 4:5],
                                         bias=bsg[:, 0:1]).then_inc(ring_copied, 1)
                else:
                    nc.scalar.activation(dst, src, ACT.Copy, scale=sg[:, w:w + 1]).then_inc(ring_copied, 1)

            def copy_kvt(i):
                act.wait_ge(kvt_turned, i + 1)
                if i >= 2:
                    act.wait_ge(kv_done, i - 1)
                nc.scalar.activation(KVT[i % 2][:].rearrange("p w a c -> p (w a c)"), PS[:, KVT_BANK, :].bitcast(BF16),
                                     ACT.Copy).then_inc(kvt_copied, 1)

            def copy_y(i):
                if i == 0:
                    act.wait_ge(y_zeroed, 1)
                for half in range(2):
                    act.wait_ge(y_done, 2 * i + half + 1)
                    for par in range(2):
                        rows = slice(64 * par, 64 * par + N)
                        src = PS[rows, Y_BANK, :].rearrange("p (i h c) -> p i h c", i=2, h=2)[:, :, par, :]
                        p0 = 4 * i + 2 * half
                        nc.scalar.activation(Y[rows, :, p0:p0 + 2].rearrange("p c i -> p i c"), src,
                                             ACT.Copy, scale=D ** -0.5).then_inc(y_copied, 1)

            def copy_perm(t, c):
                if t and c == 0:
                    act.wait_ge(hy_used, Y_PARTS * t)
                n0, n1 = PERM[c]
                act.wait_ge(perm_done, len(PERM) * t + c + 1)
                k = n1 - n0
                src = PS[:, move_bank(t, c), 0:k * B].rearrange("p (n h j) -> p n h j", n=k, h=2)
                dst = HY[:, n0:n1, :].rearrange("p n (j h) -> p n h j", h=2)
                nc.scalar.activation(dst, src, ACT.Copy, scale=sg[:, 3:4]).then_inc(perm_copied, 1)

            def gate_exponents(g):
                act.wait_ge(gate_in, g + 1)
                nc.scalar.activation(gate[:, 1], gate[:, 0], ACT.Exp).then_inc(gate_exp, 1)
                nc.scalar.activation(gate1[:, 2], gate1[:, 1], ACT.Exp).then_inc(gate_exp, 1)

            for slot in range(-1, END):
                if slot < 0:
                    spread(0, 0)
                    act.wait_ge(w_turned, 1)
                    nc.scalar.activation(wT[:].rearrange("p a c -> p (a c)"), PS[:, 0, :],
                                         ACT.Copy).then_inc(w_ready, 1)
                    act.wait_ge(sg_ready, 1)
                if 1 <= slot <= BLOCKS:
                    copy_kvt(slot - 1)
                for it in ring[slot][0]:
                    copy_item(it)
                for part in moves(slot, False):
                    copy_perm(*part)
                if 1 <= slot <= BLOCKS:
                    copy_y(slot - 1)
                for it in ring[slot][1]:
                    copy_item(it)
                for part in moves(slot, True):
                    copy_perm(*part)
                for g in gate_group(slot, 2):
                    gate_exponents(g)
                for x_ in norms(slot):
                    if x_ != (0, 0):
                        spread(*x_)
                    if x_ in ON_SCALAR:
                        scale_rows(x_[1])

            def expert_on_act(j):
                return act.value_load(piece_expert[0:1, bass.ds(j, 1)], min_val=0, max_val=E - 1)

            def gelu(j, b):
                e = expert_on_act(j)
                act.wait_ge(down_done, j + 1)
                for hb in range(HB):
                    act.wait_ge(up_done, HB * (j + AHEAD) + hb + 1)
                    nc.scalar.activation(hid[b][:, hb, :], PS[:, hb, 0:ROWS], ACT.Gelu,
                                         bias=b1c[:, bass.ds(e * HB + hb, 1)]).then_inc(gelu_done, 1)

            def set_w2(j, b):
                e = expert_on_act(j)
                act.wait_ge(down_done, j + 1)
                nc.scalar.activation(w2_now[b],
                                     W2_s[:].rearrange("p e b c -> p (e b c)")[:, bass.ds(e * HB * C, HB * C)],
                                     ACT.Copy).then_inc(w2_set, 1)

            act.wait_ge(pieces_ready, 1)
            set_w2(0, 0)
            with act.Fori(0, PIECES // DEEP - 1) as i:
                for b in range(DEEP):
                    gelu(DEEP * i + b, b % 2)
                    set_w2(DEEP * i + b + 1, (b + 1) % 2)
            for j in range(PIECES - DEEP, PIECES):
                gelu(j, j % 2)
                if j < PIECES - 1:
                    set_w2(j + 1, (j + 1) % 2)

            for g in range(G):
                act.wait_ge(shares_in[g], 16)
                for r in range(R):
                    n = R * g + r
                    m = nc.scalar.activation(shares[g][:, r, 1, :], shares[g][:, r, 1, :], ACT.Copy,
                                             scale=score[:, n, 1:2])
                m.then_inc(second_weighed, 1)

        @block.vector
        def _(v):
            steps = Steps(v, dve)
            do = steps.mark
            do(v.memset(lneps1[:], LN1_EPS))
            do(v.memset(lneps2[:], LN2_EPS))

            def chain(ins):
                steps.wait(do(ins))

            def norm_stats(phase, g):
                steps.wait(row_stats_step[0])
                s = stats[:, R * g:R * g + R, :].rearrange("p n s -> p s n")
                l = ln[:, phase, :, R * g:R * g + R]
                a = do(v.tensor_tensor(l[:, 1, :], s[:, 1, :], s[:, 4, :], ALU.subtract))
                b = do(v.tensor_tensor(l[:, 0, :], s[:, 1, :], s[:, 4, :], ALU.add))
                c = do(v.tensor_tensor(l[:, 2, :], s[:, 2, :], s[:, 5, :], ALU.add))
                steps.wait(c)
                d = do(v.tensor_tensor(l[:, 1, :], l[:, 1, :], l[:, 1, :], ALU.mult))
                chain(v.tensor_scalar(l[:, 0, :], l[:, 0, :], 0.5, None, ALU.mult))
                v.scalar_tensor_tensor(l[:, 3, :], l[:, 1, :], C / 4.0, l[:, 2, :], ALU.mult,
                                       ALU.add).then_inc(var_ready, 1)

            row_stats_step = [0]

            def row_stats(g, rows):
                for k in rows:
                    row_stats_step[0] = do(v.bn_stats(stats[:, R * g + k, :], X[:, R * g + k, :]))

            def fill(slot, st, late):
                for phase, g in norms(slot):
                    if phase == 0 and st < R and not late:
                        if st == 0:
                            v.wait_ge(x_in[g], 16)
                        row_stats(g, [st])
                    elif phase == 1 and late and st == 3:
                        add_residual(g)
                    elif phase == 1 and late and st > 3:
                        row_stats(g, range(2 * st - 8, min(2 * st - 6, R)))

            def y_part(t, part, stage):
                cols = slice(Y_PART * part, min(Y_PART * part + Y_PART, N))
                rows = lambda a: a[:, cols, :].rearrange("p n b -> p (n b)")
                if stage == 0:
                    move = next(k for k, (n0, n1) in enumerate(PERM) if cols.stop <= n1)
                    v.wait_ge(perm_copied, len(PERM) * t + move + 1)
                    y_step[0] = do(v.scalar_tensor_tensor(rows(HY), rows(VY), osg[:, 3:4], rows(HY), ALU.mult,
                                                          ALU.add))
                elif stage == 1:
                    if t >= 2:
                        v.wait_ge(ring_done, item_rank["qkv", 3, BT * (t - 1) - 1, 0] + 1)
                    steps.wait(y_step[0])
                    v.tensor_scalar(rows(ysp[t % 2]), rows(HY), 1.0, None, ALU.is_ge).then_inc(ysp_ready, 1)
                else:
                    v.scalar_tensor_tensor(rows(VY), rows(HY), 1.0, rows(HY), ALU.is_lt, ALU.mult
                                           ).then_inc(hy_used, 1)

            y_step = [0]

            def norm_spread(phase, g):
                l = ln[:, phase, :, R * g:R * g + R]
                v.wait_ge(std_ready, norm_rank[phase, g] + 1)
                v.reciprocal(l[:, 5, :], l[:, 4, :]).then_inc(rstd_ready, 1)
                if (phase, g) in ON_SCALAR:
                    v.wait_ge(rstd_ready, norm_rank[phase, g] + 1)
                    v.scalar_tensor_tensor(l[:, 1, :], l[:, 0, :], -1.0, l[:, 5, :], ALU.mult,
                                           ALU.mult).then_inc(shift_ready, 1)
                    v.wait_ge(scattered[g % SENDING], 16 * 2 * R * (g // SENDING))
                    do(v.tensor_copy(XG[g % SENDING][:, :, C], twice_token[:, R * g:R * g + R]))

            def add_residual(g):
                v.wait_ge(osp_turned, g + 1)
                rows = X[:, R * g:R * g + R, :].rearrange("p n c -> p (n c)")
                v.wait_ge(xn_ready, norm_rank[0, g] + 1)
                v.tensor_tensor(rows, PS[:, PERM_BANK, :].bitcast(BF16)[:, 0:W], rows,
                                ALU.add).then_inc(res_added, 1)
                v.wait_ge(res_added, g + 1)

            def mask_kv(i):
                v.wait_ge(kv_done, i + 1)
                if i >= 2:
                    v.wait_ge(y_done, 2 * i - 2)
                src = PS[:, KV_BANK:KV_BANK + 2, :].rearrange("p h (i c) -> p h i c", i=4)
                dst = KV[i % 2][:].rearrange("p i h c -> p h i c")
                mb = mask[:].rearrange("p h d -> p (h d)").unsqueeze(1).to_broadcast([128, 8, 128])
                mb = mb.rearrange("p (h i) c -> p h i c", h=2)
                v.tensor_tensor(dst, src, mb, ALU.mult).then_inc(kv_masked, 1)

            small = PS[:, GATE_BANK, 0:(R + 1) * E].rearrange("p (r e) -> p r e", e=E)
            lg = small[:, 0:R, :]
            rk = rank[:].unsqueeze(1).to_broadcast([128, R, E])
            bc = lambda a: a.unsqueeze(2).to_broadcast([128, R, E])

            gate_mark = {}

            def choose(g, stage):
                d, ex, t, hit1, d2, hit2 = (gate[:, k] for k in range(6))
                top, top2, e2, r1, r2, _ = (gate1[:, k] for k in range(6))
                after = lambda *names: steps.wait(max(gate_mark[n] for n in names))
                if stage == 0:
                    v.wait_ge(logits_done, g + 1)
                    gate_mark["top"] = do(v.tensor_reduce(top, lg, AX.X, ALU.max))
                elif stage == 1:
                    after("top")
                    gate_mark["d"] = do(v.tensor_tensor(d, lg, bc(top), ALU.subtract))
                elif stage == 2:
                    after("d")
                    gate_mark["t"] = do(v.scalar_tensor_tensor(t, d, 0.0, rk, ALU.is_ge, ALU.mult))
                elif stage == 3:
                    after("t")
                    gate_mark["r1"] = do(v.tensor_reduce(r1, t, AX.X, ALU.max))
                elif stage == 4:
                    after("r1")
                    gate_mark["hit1"] = do(v.tensor_tensor(hit1, t, bc(r1), ALU.is_equal))
                elif stage == 5:
                    after("hit1")
                    gate_mark["d2"] = do(v.scalar_tensor_tensor(d2, hit1, -1e30, d, ALU.mult, ALU.add))
                elif stage == 6:
                    after("d2")
                    v.tensor_reduce(top2, d2, AX.X, ALU.max).then_inc(gate_in, 1)
                elif stage == 7:
                    v.wait_ge(gate_in, g + 1)
                    gate_mark["t"] = do(v.tensor_tensor(t, d2, bc(top2), ALU.is_equal))
                elif stage == 8:
                    after("t")
                    gate_mark["t"] = do(v.tensor_tensor(t, t, rk, ALU.mult))
                elif stage == 9:
                    after("t")
                    gate_mark["r2"] = do(v.tensor_reduce(r2, t, AX.X, ALU.max))
                elif stage == 10:
                    after("r2")
                    gate_mark["hit2"] = do(v.tensor_tensor(hit2, t, bc(r2), ALU.is_equal))
                elif stage == 11:
                    after("hit2")
                    v.tensor_tensor(chosen[:, 0:R, :], hit1, hit2, ALU.add).then_inc(chosen_ready, 1)
                elif stage == 12:
                    if g >= SENDING:
                        v.wait_ge(scattered[g % SENDING], 16 * 2 * R * (g // SENDING))
                    v.tensor_copy(XG[g % SENDING][:, :, C + 1], r1).then_inc(first_ready, 1)

            def rank_rows(g, stage):
                d, ex, t, hit1, d2, hit2, t2 = (gate[:, k] for k in range(7))
                top, top2, e2, r1, r2, den = (gate1[:, k] for k in range(6))
                share = score[:, R * g:R * g + R, :]
                after = lambda *names: steps.wait(max(gate_mark[n] for n in names))
                if stage == 0:
                    v.wait_ge(ranked, g + 1)
                    gate_mark["place"] = do(v.tensor_tensor(
                        t, small[:, 0:R, :], filled[:].unsqueeze(1).to_broadcast([128, R, E]), ALU.add))
                elif stage == 1:
                    after("place")
                    gate_mark["at1"] = do(v.tensor_tensor(d2, t, hit1, ALU.mult))
                elif stage == 2:
                    gate_mark["at2"] = do(v.tensor_tensor(t2, t, hit2, ALU.mult))
                elif stage == 3:
                    if g >= SENDING:
                        v.wait_ge(scattered[g % SENDING], 16 * 2 * R * (g // SENDING))
                    after("at1")
                    with nc.allow_low_precision(reason="whole numbers below 2 ** 24"):
                        v.tensor_reduce(place[g % SENDING][:, 0, :], d2, AX.X, ALU.add).then_inc(place_ready, 1)
                elif stage == 4:
                    after("at2")
                    with nc.allow_low_precision(reason="whole numbers below 2 ** 24"):
                        v.tensor_reduce(place[g % SENDING][:, 1, :], t2, AX.X, ALU.add).then_inc(place_ready, 1)
                elif stage == 5:
                    v.tensor_tensor(filled[:], small[:, R, :], filled[:], ALU.add).then_inc(filled_ready, 1)
                elif stage == 6:
                    v.wait_ge(filled_ready, g + 1)
                    v.wait_ge(gate_exp, 2 * g + 2)
                    gate_mark["sum"] = do(v.tensor_reduce(den, ex, AX.X, ALU.add))
                elif stage == 7:
                    after("sum")
                    gate_mark["den"] = do(v.scalar_tensor_tensor(den, den, GATE_EPS, e2, ALU.mult, ALU.add))
                elif stage == 8:
                    after("den")
                    gate_mark["den"] = do(v.tensor_scalar(den, den, 1.0, None, ALU.add))
                elif stage == 9:
                    after("den")
                    gate_mark["share"] = do(v.reciprocal(share[:, :, 0], den))
                elif stage == 10:
                    after("share")
                    gate_mark["share"] = do(v.tensor_tensor(share[:, :, 1], e2, share[:, :, 0], ALU.mult))

            def gate_stage(slot, point):
                for g in gate_group(slot, 3):
                    rank_rows(g, point)
                for g in gate_group(slot, 2):
                    choose(g, point - CHOOSE_FROM)

            def first_norm():
                v.wait_ge(x_in[0], 16)
                row_stats(0, range(R))
                norm_stats(0, 0)
                v.wait_ge(lw_exp, 1)
                chain(v.tensor_scalar(osg[:], sg[:], 1.0, None, ALU.add))
                chain(v.reciprocal(sg[:], osg[:]))
                chain(v.tensor_scalar(osg[:], sg[:], -1.0, 1.0, ALU.mult, ALU.add))
                v.wait_ge(w_in, 16 * 7)
                v.tensor_tensor(bsg[:], bp_c[:], sg[:, 4:5], ALU.mult).then_inc(sg_ready, 1)
                norm_spread(0, 0)
                apply_norm(0, 0)

            def apply_norm(phase, g):
                v.wait_ge(rstd_ready, norm_rank[phase, g] + 1)
                for k in range(R):
                    n = R * g + k
                    m = v.tensor_scalar(XN[:, k, :], X[:, n, :], ln[:, phase, 0, n:n + 1],
                                        ln[:, phase, 5, n:n + 1], ALU.subtract, ALU.mult)
                    if k < R - 1:
                        do(m)
                m.then_inc(xn_ready, 1)

            def prepare_states():
                v.wait_ge(w_ready, 1)
                WpT = wT[:, 3, :]
                chain(v.tensor_copy(wpT[:, 0, :], WpT))
                chain(v.tensor_tensor(weight_rest[:, 0, :], WpT, wpT[:, 0, :], ALU.subtract))
                chain(v.tensor_copy(wpT[:, 1, :], weight_rest[:, 0, :]))
                chain(v.tensor_tensor(weight_rest[:, 1, :], weight_rest[:, 0, :], wpT[:, 1, :], ALU.subtract))
                m = do(v.tensor_copy(wpT[:, 2, :], weight_rest[:, 1, :]))
                steps.wait(m)
                do(v.memset(OM[:], 1.0))
                do(v.memset(U[:], 0.0))
                steps.wait(steps.count)
                for w, col in enumerate((0, 1, 2, 4)):
                    do(v.tensor_scalar(OM[:, w, :], OM[:, w, :], osg[:, col:col + 1], None, ALU.mult))
                v.memset(VY[:], 0.0).then_inc(wp_split, 1)
                steps.wait(steps.count)

            v.wait_ge(consts, NCONST)
            chain(v.tensor_copy(filled[:], region[:]))
            v.sem_inc(piece_read, DEEP)
            v.sem_inc(rows_ready, AHEAD)
            for slot in range(-1, END):
                if 0 <= slot < SLOTS:
                    lo = 0 if slot < BLOCKS else 3
                    hi = 4 if slot >= LAG else 3
                    h, cur = H[slot % 3], slice(lo, hi)
                    last = ("qkv", 3, slot - LAG, 0) if slot >= LAG else ("qkv", 2, slot, 0)
                    v.wait_ge(ring_copied, item_rank[last] + 1)
                    for st in range(SB):
                        if slot < BLOCKS:
                            m = do(v.tensor_tensor(h[:, cur, st, :], U[:, cur, :], h[:, cur, st, :], ALU.add))
                        else:
                            m = do(v.scalar_tensor_tensor(h[:, 3, st, :], VV[:, 3, :], osg[:, 4:5], h[:, 3, st, :],
                                                          ALU.mult, ALU.add))
                        fill(slot, st, False)
                        y_turn = slot % BT == 2 and 0 < slot // BT <= T and st < Y_PARTS
                        gate_stage(slot, 3 * st)
                        if y_turn:
                            y_part(slot // BT - 1, st, 0)
                        if st == 5 and 1 <= slot <= BLOCKS:
                            mask_kv(slot - 1)
                        steps.wait(m)
                        m = do(v.scalar_tensor_tensor(VV[:, cur, :], h[:, cur, st, :], 1.0,
                                                      h[:, cur, st, :], ALU.is_lt, ALU.mult))
                        gate_stage(slot, 3 * st + 1)
                        if y_turn:
                            y_part(slot // BT - 1, st, 1)
                        steps.wait(m)
                        if slot < BLOCKS:
                            m = do(v.tensor_tensor(U[:, cur, :], VV[:, cur, :], OM[:, cur, :], ALU.mult))
                        gate_stage(slot, 3 * st + 2)
                        if y_turn:
                            y_part(slot // BT - 1, st, 2)
                        fill(slot, st, True)
                        steps.wait(m)
                    if slot < BLOCKS:
                        if slot >= 2:
                            v.wait_ge(y_done, 2 * (slot - 1))
                        out_s = spikes[slot % 2][:, :, :, 0:N]
                        m = v.tensor_scalar(out_s, h[:, 0:3, :, :], 1.0, None,
                                            ALU.is_ge)
                        m.then_inc(block_done, 1)
                    if slot >= LAG:
                        ob = slot - LAG
                        m = v.tensor_scalar(osp[:, BC * ob:BC * ob + BC],
                                            h[:, 3].rearrange("p s n -> p (s n)"), 1.0, None, ALU.is_ge)
                        m.then_inc(osp_ready, 1)
                        if slot >= BLOCKS:
                            v.wait_ge(osp_ready, ob + 1)
                            v.sem_inc(block_done, 1)
                if slot >= SLOTS:
                    for point in range(3 * SB):
                        gate_stage(slot, point)
                if slot < 0:
                    first_norm()
                    prepare_states()
                for phase, g in norms(slot):
                    if (phase, g) == (0, 0):
                        continue
                    if not 0 <= slot < SLOTS:
                        if phase == 0:
                            v.wait_ge(x_in[g], 16)
                        else:
                            add_residual(g)
                        row_stats(g, range(R))
                    norm_stats(phase, g)
                    norm_spread(phase, g)
                    if (phase, g) in ON_VECTOR:
                        apply_norm(phase, g)

            spread_to = lambda a, n: a.unsqueeze(1).to_broadcast([128, n, E])
            chain(v.tensor_tensor(count1[:, 0], filled[:], region[:], ALU.subtract))
            chain(v.tensor_tensor(tally, counts_at[:].unsqueeze(1).to_broadcast([128, E, COUNTS]),
                                  count1[:, 0].unsqueeze(2).to_broadcast([128, E, COUNTS]), ALU.is_lt))
            chain(v.tensor_reduce(count1[:, 1], tally, AX.X, ALU.add))
            chain(v.tensor_tensor(tally[:, :, 0:E], upto[:], spread_to(count1[:, 1], E), ALU.mult))
            chain(v.tensor_reduce(count1[:, 2], tally[:, :, 0:E], AX.X, ALU.add))
            chain(v.tensor_scalar(count1[:, 3], count1[:, 1], -float(ROWS), float(CAP), ALU.mult, ALU.add))
            chain(v.tensor_tensor(passed[:, 0], piece_no[:].unsqueeze(2).to_broadcast([128, PIECES, E]),
                                  spread_to(count1[:, 2], PIECES), ALU.is_ge))
            chain(v.tensor_reduce(piece_f[:, 0], passed[:, 0], AX.X, ALU.add))
            chain(v.tensor_scalar(piece_f[:, 0], piece_f[:, 0], E - 1.0, None, ALU.min))
            chain(v.tensor_scalar(piece_rank[:], piece_f[:, 0], -1.0, float(E), ALU.mult, ALU.add))
            chain(v.tensor_copy(piece_expert[:], piece_f[:, 0]))
            chain(v.tensor_tensor(passed[:, 1], passed[:, 0], spread_to(count1[:, 3], PIECES), ALU.mult))
            chain(v.tensor_reduce(piece_f[:, 1], passed[:, 1], AX.X, ALU.add))
            chain(v.scalar_tensor_tensor(piece_f[:, 1], piece_no[:], float(ROWS), piece_f[:, 1], ALU.mult, ALU.add))
            chain(v.tensor_scalar(piece_start[:], piece_f[:, 1], float(E * CAP), None, ALU.min))
            chain(v.tensor_copy(region_end[:], filled[:]))
            v.wait_ge(ffn_in, 16 * 3)
            v.wait_ge(w_turned, 2)
            v.wait_ge(w1_in, 16)
            v.tensor_copy(b1c[:], PS[:, 1, 0:E * HB]).then_inc(pieces_ready, 1)
            v.wait_ge(pieces_ready, 1)

            def set_up(j, b):
                e = v.value_load(piece_expert[0:1, bass.ds(j, 1)], min_val=0, max_val=E - 1)
                w1 = W1_s.rearrange("p e h -> p (e h)")[:, bass.ds(e * HID, HID)]
                rows = PS[:, 6 + b % 2, 0:ROWS]
                v.wait_ge(up_done, HB * (j + 1))
                v.tensor_copy(w1_high[b % 2][:], w1).then_inc(w1_set, 1)
                v.wait_ge(piece_turned, j + 1)
                v.tensor_copy(rows_high[b % 2][:], rows).then_inc(piece_copied, 1)
                v.wait_ge(w1_set, 2 * j + 1)
                v.tensor_tensor(w1_low[b % 2][:], w1, w1_high[b % 2][:].bitcast(F32), ALU.subtract).then_inc(w1_set, 1)
                v.wait_ge(piece_copied, 2 * j + 1)
                v.tensor_tensor(rows_low[b % 2][:], rows, rows_high[b % 2][:].bitcast(F32),
                                ALU.subtract).then_inc(piece_copied, 1)

            def set_target(j, b, n):
                v.wait_ge(piece_turned, j + 1)
                if not (isinstance(n, int) and n == 0):
                    v.wait_ge(rows_sent[b], 16 * HALVES * n)
                v.scalar_tensor_tensor(target[b][:], rows_in[b][:, :, C + 1], piece_rank[:, bass.ds(j, 1)],
                                       rows_in[b][:, :, C], ALU.not_equal, ALU.add).then_inc(piece_read, 1)

            def add_b2(j, b):
                e = v.value_load(piece_expert[0:1, bass.ds(j, 1)], min_val=0, max_val=E - 1)
                v.wait_ge(down_done, AHEAD + j + 1)
                b2_e = b2b[:].rearrange("p e c -> p (e c)")[:, bass.ds(e * C, C)]
                v.tensor_tensor(rows_out[b], PS[:, 4 + b % 2, 0:ROWS].rearrange("p (a c) -> p a c", a=HALVES),
                                b2_e.unsqueeze(1).to_broadcast([128, HALVES, C]), ALU.add).then_inc(rows_ready, 1)

            def next_piece(j, b, n):
                b2, n2 = (b + AHEAD) % DEEP, n + (b + AHEAD) // DEEP
                set_up(j + AHEAD, b2)
                add_b2(j, b)
                set_target(j + AHEAD, b2, n2)

            for j in range(AHEAD):
                set_up(j, j)
                set_target(j, j, 0)
            for b in range(DEEP):
                next_piece(b, b, 0)
            with v.Fori(1, PIECES // DEEP - 1) as i:
                for b in range(DEEP):
                    next_piece(DEEP * i + b, b, i)
            for b in range(DEEP - AHEAD):
                next_piece(PIECES - DEEP + b, b, PIECES // DEEP - 1)
            for b in range(DEEP - AHEAD, DEEP):
                add_b2(PIECES - DEEP + b, b)

            for g in range(G):
                v.wait_ge(shares_in[g], 16)
                rows = X[:, R * g:R * g + R, :]
                for r in range(R):
                    n = R * g + r
                    m = do(v.scalar_tensor_tensor(X[:, n, :], shares[g][:, r, 0, :], score[:, n, 0:1], X[:, n, :],
                                                  ALU.mult, ALU.add))
                steps.wait(m)
                v.wait_ge(second_weighed, g + 1)
                v.tensor_tensor(rows, rows, shares[g][:, :, 1, :], ALU.add).then_inc(out_ready, 1)

        @block.tensor
        def _(pe):
            pe.wait_ge(consts, NCONST)
            pe.wait_ge(w_in, 16 * 7)
            for i in range(4):
                m = pe.transpose(PS[:, 0, i * 128:i * 128 + 128], wrow[:, i, :], identf[:])
            m.then_inc(w_turned, 1)
            pe.wait_ge(w_ready, 1)

            def ring_item(item):
                kind, w, b, c = item
                n = item_rank[item]
                bank = PS[:, RING + n % 2, :]
                if n >= 2:
                    pe.wait_ge(ring_copied, n - 1)
                if kind == "turn":
                    k0, k1 = CUTS[c]
                    src = XG[b % SENDING] if w else XN
                    pe.wait_ge(xn_ready, norm_rank[w, b] + 1)
                    for r in range(k0, k1):
                        m = pe.transpose(bank[:, (r - k0) * 128:(r - k0) * 128 + 128], src[:, r, 0:C], identf[:])
                    m.then_inc(ring_done, 1)
                    if c:
                        pe.wait_ge(ring_done, n + 1)
                        pe.sem_inc(xt_turned, 1)
                elif w < 3:
                    g = (BC * (b + 1) - 1) // W
                    pe.wait_ge(ring_copied, item_rank["turn", 0, g, 1] + 1)
                    pe.matmul(bank[:, 0:BC], wT[:, w, :], xT[:, BC * b:BC * b + BC], start=True,
                              stop=True).then_inc(ring_done, 1)
                else:
                    t = b // BT
                    pe.wait_ge(wp_split, 1)
                    pe.wait_ge(ysp_ready, Y_PARTS * (t + 1))
                    src = ysp[t % 2][:, :, SB * (b % BT):SB * (b % BT) + SB].rearrange("p n b -> p b n")
                    for part in range(3):
                        m = pe.matmul(bank[:, 0:BC].rearrange("p (b n) -> p b n", n=N), wpT[:, part, :], src, start=(part == 0), stop=(part == 2))
                    m.then_inc(ring_done, 1)

            def pair(w, p):
                p *= 2
                return spikes[p // SB % 2][:, w, p % SB:p % SB + 2, :].rearrange("p h n -> p (h n)")

            def turn_kv(i):
                pe.wait_ge(block_done, i + 1)
                if i:
                    pe.wait_ge(kvt_copied, i)
                bank = PS[:, KVT_BANK, :].bitcast(BF16)
                for w in range(2):
                    for a in range(4):
                        k = (w * 4 + a) * 128
                        m = pe.transpose(bank[:, k:k + 128], pair(1 + w, 4 * i + a), identb[:])
                m.then_inc(kvt_turned, 1)

            def key_value(i):
                pe.wait_ge(kvt_copied, i + 1)
                if i:
                    pe.wait_ge(kv_masked, i)
                for a in range(4):
                    for par in range(2):
                        rows = slice(64 * par, 64 * par + N)
                        m = pe.matmul(PS[:, KV_BANK + par, a * 128:a * 128 + 128], KVT[i % 2][rows, 0, a, :],
                                      KVT[i % 2][rows, 1, a, :], start=True, stop=True)
                m.then_inc(kv_done, 1)

            def query(i):
                pe.wait_ge(kv_masked, i + 1)
                for half in range(2):
                    if 2 * i + half:
                        pe.wait_ge(y_copied, 2 * (2 * i + half))
                    for a in range(2):
                        m = pe.matmul(PS[:, Y_BANK, a * 256:a * 256 + 256], pair(0, 4 * i + 2 * half + a),
                                      KV[i % 2][:, 2 * half + a, :, :].rearrange("p h c -> p (h c)"), start=True,
                                      stop=True)
                    m.then_inc(y_done, 1)

            perm_bank_users = [0, 0]

            def permute(t, c):
                pe.wait_ge(y_copied, 4 * BT * (t + 1))
                bank = move_bank(t, c)
                if bank == PERM_BANK:
                    if perm_bank_users[0]:
                        pe.wait_ge(perm_copied, perm_bank_users[0])
                    if perm_bank_users[1]:
                        pe.wait_ge(res_added, perm_bank_users[1])
                perm_bank_users[0] += 1
                n0, n1 = PERM[c]
                for n in range(n0, n1):
                    chans = range(128 * n // N, (128 * n + 127) // N + 1)
                    for par in range(2):
                        col = ((n - n0) * 2 + par) * (B // 2)
                        for ch in chans:
                            s = N * ch - 128 * n
                            m = pe.matmul(PS[:, bank, col:col + B // 2], shift[:, par, 127 - s:255 - s],
                                          Y[:, ch, t * B // 2:(t + 1) * B // 2], start=(ch == chans[0]),
                                          stop=(ch == chans[-1]))
                m.then_inc(perm_done, 1)

            def turn_out(g):
                pe.wait_ge(osp_ready, norm2_block(g) + 1)
                if perm_bank_users[0]:
                    pe.wait_ge(perm_copied, perm_bank_users[0])
                if perm_bank_users[1]:
                    pe.wait_ge(res_added, perm_bank_users[1])
                perm_bank_users[1] += 1
                for r in range(R):
                    k = R * g + r
                    m = pe.transpose(PS[:, PERM_BANK, :].bitcast(BF16)[:, r * 128:r * 128 + 128],
                                     osp[:, k * 128:k * 128 + 128], identb[:])
                m.then_inc(osp_turned, 1)

            small = PS[:, GATE_BANK, 0:(R + 1) * E].rearrange("p (r e) -> p r e", e=E)

            def logits(g):
                pe.wait_ge(ring_copied, item_rank["turn", 1, g, 1] + 1)
                if g:
                    pe.wait_ge(filled_ready, g)
                for r in range(R):
                    n = R * g + r
                    m = pe.matmul(small[:, r, :], xT[:, n * 128:n * 128 + 128], Wg_s[:], start=True, stop=True)
                m.then_inc(logits_done, 1)

            def count_before(g):
                pe.wait_ge(chosen_ready, g + 1)
                pe.matmul(small, before[:], chosen[:], start=True, stop=False)
                for r in range(R):
                    m = pe.matmul(small[:, r + 1:R + 1, :], all_ones[:],
                                  chosen[:, r:r + 1, :].to_broadcast([128, R - r, E]), start=False, stop=(r == R - 1))
                m.then_inc(ranked, 1)

            pe.sem_inc(up_done, AHEAD * HB)
            pe.sem_inc(down_done, AHEAD)
            for slot in range(-1, END):
                for phase, g in norms(slot):
                    if phase:
                        turn_out(g)
                for g in gate_group(slot, 2):
                    if slot > BLOCKS:
                        logits(g)
                if 1 <= slot <= BLOCKS:
                    turn_kv(slot - 1)
                for it in ring[slot][0]:
                    ring_item(it)
                for part in moves(slot, False):
                    permute(*part)
                if 1 <= slot <= BLOCKS:
                    key_value(slot - 1)
                    query(slot - 1)
                for it in ring[slot][1]:
                    ring_item(it)
                for part in moves(slot, True):
                    permute(*part)
                for g in gate_group(slot, 1):
                    if slot < BLOCKS:
                        logits(g)
                for g in gate_group(slot, 2):
                    count_before(g)

            pe.wait_ge(ffn_in, 16 * 3)
            pe.wait_ge(ring_copied, len(item_rank))
            pe.transpose(PS[:, 1, 0:E * HB], b1r[:], identf[0:E * HB, 0:E * HB]).then_inc(w_turned, 1)

            def turn_piece(j, b, n):
                pe.wait_ge(piece_in[b], 16 * (n + 1))
                for a in range(HALVES):
                    m = pe.transpose(PS[:, 6 + b % 2, a * 128:a * 128 + 128], rows_in[b][:, a, 0:C], identf[:])
                m.then_inc(piece_turned, 1)

            def up(j, b, after_first=True):
                pe.wait_ge(w1_set, 2 * j + 2)
                pe.wait_ge(piece_copied, 2 * j + 2)
                for hb in range(HB):
                    if after_first:
                        pe.wait_ge(gelu_done, HB * (j - 1) + hb + 1)
                    cols = slice(hb * 128, hb * 128 + 128)
                    high, low = w1_high[b % 2][:, cols], w1_low[b % 2][:, cols]
                    rows, rows_l = rows_high[b % 2][:], rows_low[b % 2][:]
                    pe.matmul(PS[:, hb, 0:ROWS], high, rows, start=True, stop=False)
                    pe.matmul(PS[:, hb, 0:ROWS], high, rows_l, start=False, stop=False)
                    pe.matmul(PS[:, hb, 0:ROWS], low, rows, start=False, stop=True).then_inc(up_done, 1)

            def down(j, b):
                pe.wait_ge(w2_set, j + 1)
                pe.wait_ge(rows_ready, j + 1)
                pe.wait_ge(gelu_done, HB * (j + 1))
                for a in range(HALVES):
                    for hb in range(HB):
                        m = pe.matmul(PS[:, 4 + b % 2, a * 128:a * 128 + 128], hid[b % 2][:, hb, a * 128:a * 128 + 128],
                                      w2_now[b % 2][:, hb * C:hb * C + C], start=(hb == 0), stop=(hb == HB - 1))
                m.then_inc(down_done, 1)

            turn_piece(0, 0, 0)
            turn_piece(1, 1, 0)
            up(0, 0, after_first=False)

            def next_products(j, b, n):
                turn_piece(j + AHEAD, (b + AHEAD) % DEEP, n + (b + AHEAD) // DEEP)
                up(j + 1, (b + 1) % DEEP)
                down(j, b)

            with pe.Fori(0, PIECES // DEEP - 1) as i:
                for b in range(DEEP):
                    next_products(DEEP * i + b, b, i)
            for b in range(DEEP - AHEAD):
                next_products(PIECES - DEEP + b, b, PIECES // DEEP - 1)
            up(PIECES - 1, DEEP - 1)
            down(PIECES - 2, DEEP - 2)
            down(PIECES - 1, DEEP - 1)


_INS = ["x", "L0_conv_Wq", "L0_conv_Wk", "L0_conv_Wv", "L0_conv_Wp", "L0_conv_bp", "lif_w", "L0_ffn_Wg",
        "L0_ffn_W1", "L0_ffn_b1", "L0_ffn_W2", "L0_ffn_b2"]


def kernel(**inputs):
    import numpy as np
    import concourse.bacc as bacc
    from concourse import mybir as mb
    from concourse.bass_utils import run_bass_kernel_spmd

    lifs = [np.reshape(inputs[f"L0_conv_{n}"], (1,)) for n in ("wq", "wk", "wv", "wa", "wp")]
    inputs = {**inputs, "lif_w": np.concatenate(lifs)}
    nc = bacc.Bacc("TRN2", target_bir_lowering=False, num_devices=1)
    arrays, args = {}, []
    for name in _INS:
        a = np.ascontiguousarray(inputs[name])
        arrays[f"in_{name}"] = a
        args.append(nc.dram_tensor(f"in_{name}", a.shape, mb.dt.from_np(a.dtype), kind="ExternalInput").ap())
    out = nc.dram_tensor("out", inputs["x"].shape, mb.dt.float32, kind="ExternalOutput").ap()
    metaformer_block(nc, *args, out)
    r = run_bass_kernel_spmd(nc, [arrays], core_ids=[0])
    return r.results[0]["out"]
```
